# Optimizing a Trainium2 kernel written in Bass

```python
import numpy as np
import jax
import jax.numpy as jnp

def _softmax(x, axis=-1):
    return jax.nn.softmax(x, axis=axis)

def _gelu(x):
    return jax.nn.gelu(x, approximate=True)

def _silu(x):
    return jax.nn.silu(x)

def _sigmoid(x):
    return jax.nn.sigmoid(x)

def _layernorm(x, axis=-1, eps=1e-05):
    m = jnp.mean(x, axis=axis, keepdims=True)
    v = jnp.var(x, axis=axis, keepdims=True)
    return (x - m) / jnp.sqrt(v + eps)

def _scatter_add(tgt, idx, src, axis=0):
    return tgt.at[idx].add(src)

def _segment_sum(src, seg, n):
    return jax.ops.segment_sum(src, seg, n)
kernel_name = 'mk_flamingo_gated_d1_seqx_r4_f0c29f'

def setup_inputs(seed: int=0):
    np.random.seed(seed)
    _w = jnp.asarray

    def _rec_inputs():
        import jax
        import jax.numpy as jnp
        _rk = jax.random.key(seed)
        x = 7.22e-05 + 1 * jax.random.normal(jax.random.fold_in(_rk, 1), (64, 128, 512), jnp.float32)
        _lenS = 128 - jax.random.randint(jax.random.fold_in(_rk, 7), (64,), 0, max(1, 128 // 4) + 1, jnp.int32)
        _lenS2 = 128 - jax.random.randint(jax.random.fold_in(_rk, 8), (64,), 0, max(1, 128 // 4) + 1, jnp.int32)
        _ctx_2048P = jax.random.normal(jax.random.fold_in(_rk, 11), (64, 16, 512), jnp.float32)
        _ctx_2048c = jax.random.dirichlet(jax.random.fold_in(_rk, 511), 0.3 * jnp.ones((16,), jnp.float32), (64, 128))
        _ctx_2048t = jnp.einsum('bsk,bkd->bsd', _ctx_2048c, _ctx_2048P)
        _ctx_2048t = _ctx_2048t * jax.lax.rsqrt(jnp.mean(jnp.square(_ctx_2048t)) + 1e-12) * 0.953939
        ctx_2048 = 4.13588e-05 + 0.999923 * (_ctx_2048t + 0.3 * jax.random.normal(jax.random.fold_in(_rk, 611), (64, 128, 512), jnp.float32))
        _g = jax.random.normal(jax.random.fold_in(_rk, 9001), (2, 1), jnp.float32)
        _g = jnp.sign(_g) * jnp.maximum(jnp.abs(_g), 1.0) + (_g == 0) * 1.0
        g_xattn = _g[0]
        g_ffn = _g[1]
        return (x, ctx_2048, g_xattn, g_ffn)
    x, ctx_2048, g_xattn, g_ffn = _rec_inputs()

    def _L0_xattn_setup():
        import jax, jax.numpy as jnp
        import numpy as np
        B, S, DIM, HD = (4, 256, 512, 128)
        H = DIM // HD
        GN_EPS = 0.001

        def _decay_masks(n_heads, seq_len):
            gam = 1.0 - 2.0 ** (-5.0 - jnp.arange(n_heads, dtype=jnp.float32))
            idx = jnp.arange(seq_len, dtype=jnp.float32)
            expo = idx[None, :] - idx[:, None]
            D = jnp.where(expo[None, :, :] <= 0, gam[:, None, None] ** expo[None, :, :], 0.0)
            return D / jnp.sqrt(D.sum(axis=-1))[:, None, :]
        key = jax.random.key(seed)
        ks = jax.random.split(key, 8)
        x = jax.random.normal(ks[0], (B, S, DIM), dtype=jnp.float32)
        k = jax.random.normal(ks[1], (B, S, DIM), dtype=jnp.float32)
        v = jax.random.normal(ks[2], (B, S, DIM), dtype=jnp.float32)
        Wh = jax.random.normal(ks[3], (H, HD, HD), dtype=jnp.float32) / np.sqrt(HD)
        wg_w = jax.random.normal(ks[4], (DIM, DIM), dtype=jnp.float32) / np.sqrt(DIM)
        wo_w = jax.random.normal(ks[5], (DIM, DIM), dtype=jnp.float32) / np.sqrt(DIM)
        gn_gamma = jnp.ones((DIM,), dtype=jnp.float32)
        gn_beta = jnp.zeros((DIM,), dtype=jnp.float32)
        return {'x': x, 'k': k, 'v': v, 'Wh': Wh, 'wg_w': wg_w, 'wo_w': wo_w, 'gn_gamma': gn_gamma, 'gn_beta': gn_beta}
    _L0_xattn_all = _L0_xattn_setup()
    _L0_xattn_in = {k: v for k, v in _L0_xattn_all.items() if k in ('Wh', 'wg_w', 'wo_w', 'gn_gamma', 'gn_beta')}
    del _L0_xattn_all

    def _L0_ffn_setup():
        import jax, jax.numpy as jnp
        import numpy as np
        HIDDEN = 512
        INTER = 1408
        B, S = (2, 512)

        def _ternary(key, shape):
            return jax.random.randint(key, shape, -1, 2).astype(jnp.float32)
        key = jax.random.key(seed)
        ks = jax.random.split(key, 7)
        x = jax.random.normal(ks[0], (B, S, HIDDEN), dtype=jnp.float32)
        gate_w = _ternary(ks[1], (INTER, HIDDEN))
        up_w = _ternary(ks[2], (INTER, HIDDEN))
        down_w = _ternary(ks[3], (HIDDEN, INTER))
        gate_s = jax.random.uniform(ks[4], (INTER,), minval=0.01, maxval=0.1, dtype=jnp.float32)
        up_s = jax.random.uniform(ks[5], (INTER,), minval=0.01, maxval=0.1, dtype=jnp.float32)
        down_s = jax.random.uniform(ks[6], (HIDDEN,), minval=0.01, maxval=0.1, dtype=jnp.float32)
        return {'x': x, 'gate_w': gate_w, 'up_w': up_w, 'down_w': down_w, 'gate_s': gate_s, 'up_s': up_s, 'down_s': down_s}
    _L0_ffn_all = _L0_ffn_setup()
    _L0_ffn_in = {k: v for k, v in _L0_ffn_all.items() if k in ('gate_w', 'up_w', 'down_w', 'gate_s', 'up_s', 'down_s')}
    del _L0_ffn_all
    return {'x': x, 'ctx_2048': ctx_2048, 'g_xattn': g_xattn, 'g_ffn': g_ffn, 'L0_xattn_Wh': _L0_xattn_in['Wh'], 'L0_xattn_wg_w': _L0_xattn_in['wg_w'], 'L0_xattn_wo_w': _L0_xattn_in['wo_w'], 'L0_xattn_gn_gamma': _L0_xattn_in['gn_gamma'], 'L0_xattn_gn_beta': _L0_xattn_in['gn_beta'], 'L0_ffn_gate_w': _L0_ffn_in['gate_w'], 'L0_ffn_up_w': _L0_ffn_in['up_w'], 'L0_ffn_down_w': _L0_ffn_in['down_w'], 'L0_ffn_gate_s': _L0_ffn_in['gate_s'], 'L0_ffn_up_s': _L0_ffn_in['up_s'], 'L0_ffn_down_s': _L0_ffn_in['down_s']}

def reference(x, ctx_2048, g_xattn, g_ffn, L0_xattn_Wh, L0_xattn_wg_w, L0_xattn_wo_w, L0_xattn_gn_gamma, L0_xattn_gn_beta, L0_ffn_gate_w, L0_ffn_up_w, L0_ffn_down_w, L0_ffn_gate_s, L0_ffn_up_s, L0_ffn_down_s):
    import jax
    import jax.numpy as jnp

    def _L0_xattn_ref(x, k, v, Wh, wg_w, wo_w, gn_gamma, gn_beta):
        import jax, jax.numpy as jnp
        import numpy as np
        B, S, DIM, HD = (4, 256, 512, 128)
        H = DIM // HD
        GN_EPS = 0.001

        def _decay_masks(n_heads, seq_len):
            gam = 1.0 - 2.0 ** (-5.0 - jnp.arange(n_heads, dtype=jnp.float32))
            idx = jnp.arange(seq_len, dtype=jnp.float32)
            expo = idx[None, :] - idx[:, None]
            D = jnp.where(expo[None, :, :] <= 0, gam[:, None, None] ** expo[None, :, :], 0.0)
            return D / jnp.sqrt(D.sum(axis=-1))[:, None, :]
        b, s, dim = x.shape
        h, hd, _ = Wh.shape
        xh = x.reshape(b, s, h, hd)
        kh = k.reshape(b, s, h, hd)
        vh = v.reshape(b, s, h, hd)
        Q = jnp.einsum('bshd,hde->bshe', xh, Wh)
        K = jnp.einsum('bshd,hde->bshe', kh, Wh)
        V = jnp.einsum('bshd,hde->bshe', vh, Wh)
        scores = jnp.einsum('bshe,bthe->bhst', Q, K) / jnp.sqrt(jnp.float32(hd))
        Dn = _decay_masks(h, s)
        masked = scores * Dn[None, :, :, :]
        A = jnp.maximum(jnp.abs(masked.sum(axis=0)), 1.0)
        O = jnp.einsum('hst,bthe->bshe', A, V).reshape(b, s, dim)
        mu = O.mean(axis=-1, keepdims=True)
        var = O.var(axis=-1, keepdims=True)
        Y = (O - mu) / jnp.sqrt(var + GN_EPS) * gn_gamma + gn_beta
        W = jax.nn.relu(x @ wg_w)
        return W * Y @ wo_w

    def _L0_ffn_ref(x, gate_w, up_w, down_w, gate_s, up_s, down_s):
        import jax, jax.numpy as jnp
        import numpy as np
        HIDDEN = 512
        INTER = 1408
        B, S = (2, 512)

        def _ternary(key, shape):
            return jax.random.randint(key, shape, -1, 2).astype(jnp.float32)
        b, s, h = x.shape
        xf = x.reshape(b * s, h)
        g = jnp.einsum('th,ih->ti', xf, gate_w) * gate_s
        u = jnp.einsum('th,ih->ti', xf, up_w) * up_s
        hdn = jax.nn.silu(g) * u
        out = jnp.einsum('ti,hi->th', hdn, down_w) * down_s
        return out.reshape(b, s, -1)
    x = x + jnp.tanh(g_xattn[0]) * _L0_xattn_ref(_layernorm(x, axis=-1), ctx_2048, ctx_2048, L0_xattn_Wh, L0_xattn_wg_w, L0_xattn_wo_w, L0_xattn_gn_gamma, L0_xattn_gn_beta)
    x = x + jnp.tanh(g_ffn[0]) * _L0_ffn_ref(_layernorm(x, axis=-1), L0_ffn_gate_w, L0_ffn_up_w, L0_ffn_down_w, L0_ffn_gate_s, L0_ffn_up_s, L0_ffn_down_s)
    return x

_drawn_inputs = setup_inputs


def setup_inputs(seed=0):
    import zlib

    import numpy as np

    out = dict(_drawn_inputs(seed))
    spreads = {'L0_xattn_gn_gamma': (1.0, 0.2), 'L0_xattn_gn_beta': (0.0, 0.1)}
    factors = {}
    for name, (base, spread) in spreads.items():
        noise = np.random.default_rng([zlib.crc32(name.encode()), seed]).standard_normal(out[name].shape)
        drawn = base * np.exp(spread * noise) if base else spread * noise
        out[name] = jnp.asarray(drawn.astype(out[name].dtype))
    for name, factor in factors.items():
        out[name] = (out[name] * factor).astype(out[name].dtype)
    return out
```

```python
import numpy as np
import concourse.bass as bass
from concourse import mybir
from contextlib import ExitStack

B, S, D, H, HD, NI = 64, 128, 512, 4, 128, 11
INTER = NI * 128
NG = B // 4
LATE = NG - 2


class Plan:

    def __init__(self):
        self.queue, self.total, self.value = {}, {}, {}

    def do(self, engine, make, after=(), then=None, inc=1):
        if then is not None:
            kind = then[0]
            self.total[kind] = self.total.get(kind, 0) + inc
            assert then not in self.value
            self.value[then] = self.total[kind]
        self.queue.setdefault(engine, []).append((tuple(after), make, then, inc))

    def emit(self, name, engine, sems, seen, *args):
        for after, make, then, inc in self.queue.get(name, ()):
            for event in after:
                value = self.value[event]
                if seen.get(event[0], 0) < value:
                    seen[event[0]] = value
                    engine.wait_ge(sems[event[0]], value)
            made = make(engine, *args)
            if then is not None:
                made.then_inc(sems[then[0]], inc)


def gated_layer(nc, x, ctx_t, wh, wh_t, wg, wo, gate_t, up_t, down_t, cols, rows, decay, eye, out):
    f32, f32r, u32, i32 = mybir.dt.float32, mybir.dt.float32r, mybir.dt.uint32, mybir.dt.int32
    ALU = mybir.AluOpType
    ACT = mybir.ActivationFunctionType
    AX = mybir.AxisListType

    stack = ExitStack()
    with stack:
        def sb(name, shape, dt=f32):
            return stack.enter_context(nc.sbuf_tensor(name, shape, dt))

        gate = sb("gate", [128, 4, INTER], f32r)
        up = sb("up", [128, 4, INTER], f32r)
        xreg = sb("xreg", [128, 12 * 512], f32r)
        wgs = [xreg[:, 2048 * i:2048 * i + 2048].rearrange("p (k n) -> p k n", k=4) for i in range(2)]
        gs_ = [xreg[:, 4096 + 512 * i:4608 + 512 * i].rearrange("p (h n) -> p h n", h=4) for i in range(2)]
        whs = xreg[:, 5120:6144].rearrange("p (h q n) -> p h q n", h=4, q=2)
        down = xreg[:, 0:NI * 512].rearrange("p (i n) -> p i n", i=NI)
        a_lo_t = sb("a_lo", [128, 512], f32r)
        a_parts = [xreg[:, 5632:6144].rearrange("p (h n) -> p h n", h=4),
                   a_lo_t[:, :].rearrange("p (h n) -> p h n", h=4)]
        reg = sb("reg", [128, 84 * 256], f32r)

        def part(kib, n, **dims):
            v = reg[:, 256 * kib:256 * kib + n * int(np.prod(list(dims.values())))]
            names = list(dims)
            return v.rearrange(f"p ({' '.join(names)} n) -> p {' '.join(names)} n", **dims)

        xnt = [[part(16 * b + 8 * i, 512, k=4) for i in range(2)] for b in range(2)]
        zt = part(32, 512, q=2, h=4)
        ct = [[part(48 + 16 * b + 8 * i, 512, h=4) for i in range(2)] for b in range(2)]
        hid = [part(22 * i, 512, i=NI) for i in range(2)]
        vs = [part(44 + 4 * i, 512, b=2) for i in range(2)]
        x2t = [part(52 + 8 * i, 512, k=4) for i in range(2)]
        wos = [part(68 + 8 * i, 512, k=4) for i in range(2)]
        wyt = [sb(f"wyt{i}", [128, 4, 128], f32r) for i in range(2)]

        xr = sb("xr", [128, 8, 512])
        xn = sb("xn", [128, 2, 512])
        tmp = sb("tmp", [128, 4, 512])
        raw = sb("raw", [128, 4, 512])
        stg = sb("stg", [128, 704])
        colsb = sb("colsb", [128, 2 * NI + 2])
        rowsb = sb("rowsb", [128, 3, 512])
        ident = sb("ident", [128, 128])
        tg = sb("tg", [128, 2])
        st = sb("st", [128, 4, 6])
        mv = sb("mv", [128, 8, 2])
        rs = sb("rs", [128, 8])
        st2 = sb("st2", [128, 4, 6])
        mv2 = sb("mv2", [128, 8, 2])
        rs2 = sb("rs2", [128, 8])
        low = sb("low", [128, 24])
        lowm = sb("lowm", [128, 1])
        ones = sb("ones", [128, 1])
        nhalf = sb("nhalf", [128, 1])
        flag = sb("flag", [1, 1], i32)
        gamma, beta, ds = rowsb[:, 0, :], rowsb[:, 1, :], rowsb[:, 2, :]
        yb = tmp[:, 3, :]

        ps = [stack.enter_context(nc.psum_tensor(f"ps{i}", [128, 4, 2, 128], f32)) for i in range(2)]
        pv, psc = ps
        banks = [p[:, 2 * i:2 * i + 2, :, :].rearrange("p a b n -> p (a b n)") for p in ps for i in range(2)]
        po = stack.enter_context(nc.psum_tensor("po", [128, 2, 2, 256], f32))
        ptb = stack.enter_context(nc.psum_tensor("ptb", [128, 4, 128], f32))
        pyb = stack.enter_context(nc.psum_tensor("pyb", [128, 512], f32))
        pz = [po[:, i, :, :].rearrange("p a n -> p (a n)") for i in range(2)]

        v_s = nc.dram_tensor("v_scratch", [128, B, D], f32, kind="Internal").ap()
        w_s = nc.dram_tensor("w_scratch", [128, B, D], f32, kind="Internal").ap()
        gate_s = nc.dram_tensor("gate_scratch", [D, INTER], f32, kind="Internal").ap()
        up_s = nc.dram_tensor("up_scratch", [D, INTER], f32, kind="Internal").ap()
        down_s = nc.dram_tensor("down_scratch", [INTER, D], f32, kind="Internal").ap()

        x_v = x.rearrange("b s d -> s b d")
        out_v = out.rearrange("b s d -> s b d")
        ct_v = ctx_t.rearrange("(h p) n -> p h n", p=128)
        down_flat = down_t.rearrange("(p a) n -> p (a n)", p=128)

        plan = Plan()
        do = plan.do

        def f(ap):
            return ap.bitcast(f32)

        def dma(key, dst, src, after=()):
            do("sp", lambda e: e.dma_start(dst, src), after, key, 16)

        def high(key, dst, src, after):
            do("act", lambda e: e.copy(dst, src), after, key)

        def rest(key, dst, src, hi, after):
            do("dve", lambda e: e.tensor_tensor(dst, src, f(hi), ALU.subtract), after, key)

        def three(e, dst, lhs, rhs, k, n, sl=slice(None), sr=slice(None), **kw):
            for i, (a, b) in enumerate(((0, 0), (0, 1), (1, 0))):
                last = e.matmul(dst, lhs[a][sl], rhs[b][sr], start=(k == 0 and i == 0),
                                stop=(k == n - 1 and i == 2), **kw)
            return last

        def x_load(q):
            after = [("xn", 2 * q - 7)] if q >= 4 else []
            if q == 3:
                after = [("whlo", 0), ("G", 0)]
            dma((f"xl{q % 4}", q), xr[:, 2 * q % 8:2 * q % 8 + 2, :], x_v[:, 2 * q:2 * q + 2, :], after)

        def stats(t):
            do("dve", lambda e: e.bn_stats(st[:, t % 4, :], xr[:, t % 8, :]), [(f"xl{t // 2 % 4}", t // 2)], ("st", t))
            do("dve", lambda e: e.bn_aggr(mv[:, t % 8, :], st[:, t % 4, :]), [("st", t)], ("mv", t))

        def power(key, dst, var, eps, after):
            do("pool", lambda e: e.tensor_scalar(dst, var, eps, None, ALU.add), after, ("eps", key))
            do("pool", lambda e: e.tensor_tensor(dst, dst, nhalf[:, :], ALU.pow), [("eps", key), ("ones", 1)], key)

        def rstd(t):
            power(("rs", t), rs[:, t % 8:t % 8 + 1], mv[:, t % 8, 1:2], 1e-5, [("mv", t)])

        def norm(t):
            after = [("rs", t), ("mv", t)] + ([("tb", ("x", t - 2))] if t >= 2 else [])
            do("dve", lambda e: e.tensor_scalar(xn[:, t % 2, :], xr[:, t % 8, :], mv[:, t % 8, 0:1],
                                                rs[:, t % 8:t % 8 + 1], ALU.subtract, ALU.mult), after, ("xn", t))

        tb_last = [None]

        def transpose(q, key, src, after):
            if tb_last[0] is not None:
                after = [*after, ("tbe", tb_last[0])]
            tb_last[0] = key

            def make(e, *_):
                for k in range(4):
                    last = e.transpose(ptb[:, k, :], src[:, 128 * k:128 * k + 128], ident[:, :])
                return last
            do(q, make, after, ("tb", key))

        def transposed_hi(key, dst, after=()):
            high(("tbh", key), dst, ptb[:, :, :], [("tb", key), *after])

        def transposed_lo(key, dst, hi):
            rest(("tbe", key), dst, ptb[:, :, :], hi, [("tbh", key)])

        def xt_dst(t):
            return [p[:, :, 128 * (t % 4):128 * (t % 4) + 128] for p in xnt[t // 4 % 2]]

        def xt(t):
            transpose("pe", ("x", t), xn[:, t % 2, :], [("xn", t), ("c", "eye")])

        def xt_hi(t):
            transposed_hi(("x", t), xt_dst(t)[0])

        def xt_lo(t):
            transposed_lo(("x", t), xt_dst(t)[1], xt_dst(t)[0])

        def z(g, h):
            after = [("tbe", ("x", 4 * g + 3)), ("Glo", 0)]
            n = 4 * g + h
            if n >= 2:
                after.append(("zlo", n - 2))
            do("pe", lambda e, *_: three(e, pz[h % 2], gs_, xnt[g % 2], 0, 1, (slice(None), h, slice(None)),
                                         (slice(None), h, slice(None))), after, ("z", n))

        def z_hi(g, h):
            high(("zhi", 4 * g + h), zt[:, 0, h, :], pz[h % 2], [("z", 4 * g + h)])

        def z_lo(g, h):
            rest(("zlo", 4 * g + h), zt[:, 1, h, :], pz[h % 2], zt[:, 0, h, :], [("zhi", 4 * g + h)])

        def ct_load(g, hp):
            after = [("ctlo", (g - 1, 2 * hp + 1))] if g else []
            dma((f"ct{hp}", g), raw[:, 2 * hp:2 * hp + 2, :], ct_v[:, 2 * hp:2 * hp + 2, 512 * g:512 * g + 512], after)

        def ct_split(g, h, first=False):
            a, b = ct[g % 2][0][:, h, :], ct[g % 2][1][:, h, :]
            after = [(f"ct{h // 2}", g)] + ([("s", (g - 2, 3))] if g >= 2 else [])
            do("act" if first else "pool", lambda e: (e.copy if first else e.tensor_copy)(a, raw[:, h, :]),
               after, ("cthf" if first else "cthi", (g, h)))
            do("dve" if first else "pool", lambda e: e.tensor_tensor(b, raw[:, h, :], f(a), ALU.subtract),
               [("cthf" if first else "cthi", (g, h))], ("ctlo", (g, h)) if not first else ("ctlf", (g, h)))

        def v(t):
            g, b = divmod(t, 4)
            after = [("ctlo", (0, 3)), ("ctlf", (0, 1))] if g == 0 else [("ctlo", (g, 3))]
            after += [("whlo", 0)] + ([("vev", t - 1)] if t else [])

            def make(e, *_):
                for h in range(4):
                    for i in range(2):
                        last = e.matmul(pv[:, h, :, :], ct[g % 2][i][:, h, 128 * b:128 * b + 128], whs[:, h, :, :],
                                        start=(i == 0), stop=(i == 1))
                return last
            do("pe", make, after, ("v", t))

        def v_out(t):
            dst = tmp[:, 2 + t % 2, :].rearrange("p (h n) -> p h n", h=4)
            after = [("v", t)] + ([(f"vst{t % 2}", t - 2)] if t >= 2 else [("wglo", 2 + t)])
            do("act", lambda e: e.copy(dst, pv[:, :, 1, :]), after, ("vlow", t))
            do("dve", lambda e: e.tensor_tensor(dst, pv[:, :, 0, :], dst, ALU.add), [("vlow", t)], ("vev", t))

        def v_store(t):
            dma((f"vst{t % 2}", t), v_s[:, t, :], tmp[:, 2 + t % 2, :], [("vev", t)])

        def pw(t):
            return pyb[:, :] if t < 4 * LATE else banks[t % 2]

        def w(t):
            after = [("tbe", ("x", t)), ("wglo", 3)] + ([("wev", t - (2 if t > 4 * LATE else 1))] if t else [])

            def make(e, *_):
                sl = slice(128 * (t % 4), 128 * (t % 4) + 128)
                for k in range(4):
                    last = three(e, pw(t), xnt[t // 4 % 2], wgs, k, 4, (slice(None), k, sl),
                                 (slice(None), k, slice(None)))
                return last
            do("pe", make, after, ("w", t))

        def w_out(t):
            after = [("w", t)] + ([(f"wst{t % 2}", t - 2)] if t >= 2 else [("wglo", t)])
            do("act", lambda e: e.activation(tmp[:, t % 2, :], pw(t), ACT.Relu), after, ("wev", t))

        def w_store(t):
            dma((f"wst{t % 2}", t), w_s[:, t, :], tmp[:, t % 2, :], [("wev", t)])

        def scores(g, h):
            def make(e, *_):
                for b in range(4):
                    sl = slice(128 * b, 128 * b + 128)
                    for i in range(2):
                        last = e.matmul(psc[:, h, :, :], ct[g % 2][i][:, h, sl], zt[:, :, h, sl],
                                        start=(g == 0 and h % 2 == 0 and b == 0 and i == 0),
                                        stop=(g == NG - 1 and h % 2 == 1 and b == 3 and i == 1), skip_group_check=True)
                return last
            do("pe", make, [("zlo", 4 * g + h)], ("s", (g, h)))

        chunks = ([(gate_t[128 * k:128 * k + 128, :], gate_s[128 * k:128 * k + 128, :], gate[:, k, :]) for k in range(4)]
                  + [(up_t[128 * k:128 * k + 128, :], up_s[128 * k:128 * k + 128, :], up[:, k, :]) for k in range(4)]
                  + [(down_t[352 * k:352 * k + 352, :], down_s[352 * k:352 * k + 352, :], None) for k in range(4)])

        def to_scratch(c):
            src, dst, _ = chunks[c]
            dma((f"scr{c}", 0), dst, src)

        def weight_load(c):
            _, src, dst = chunks[c]
            dma((f"wld{c}", 0), f(dst), src, [(f"scr{c}", 0)])

        def low_load(c, half):
            at = 1408 * (c - 8) + 704 * half
            after = [("low", 2 * c + half - 1)]
            dma(("lowld", 2 * c + half), stg[:, :], down_flat[:, at:at + 704], after)

        def low_bits(c, half):
            n = 2 * c + half
            if c < 8:
                src, after = chunks[c][2][:, 704 * half:704 * half + 704].bitcast(u32), [(f"wld{c}", 0)]
            else:
                src, after = stg[:, :].bitcast(u32), [("lowld", n)]
            do("dve", lambda e: e.tensor_scalar(stg[:, :].bitcast(u32), src, 0xFFF, None, ALU.bitwise_and), after,
               ("and", n))
            do("dve", lambda e: e.tensor_reduce(low[:, n:n + 1], stg[:, :].bitcast(i32), AX.X, ALU.max),
               [("and", n)], ("low", n))

        dma(("xl0", 0), xr[:, 0:2, :], x_v[:, 0:2, :])
        dma(("c", "eye"), ident[:, :], eye)
        x_load(1)
        dma(("whr", 0), xr[:, 6, :].rearrange("p (h n) -> p h n", h=4), wh_t.rearrange("h e d -> e h d"))
        ct_load(0, 1)
        ct_load(0, 0)
        dma(("whr2", 0), xr[:, 7, :].rearrange("p (h n) -> p h n", h=4), wh.rearrange("h d e -> d h e"))
        x_load(2)
        dma(("wgr", 0), tmp[:, :, :], wg.rearrange("(k p) n -> p k n", p=128))
        x_load(3)
        dma(("cols", 0), colsb[:, :], cols)
        dma(("rows", 0), rowsb[:, :, :], rows)

        do("pool", lambda e: e.memset(ones[:, :], 1.0), (), ("ones", 0))
        do("pool", lambda e: e.memset(nhalf[:, :], -0.5), (), ("ones", 1))

        for t in range(2):
            stats(t)
            rstd(t)
        for t in range(4):
            norm(t)
            if t < 3:
                stats(t + 2)
                rstd(t + 2)
            xt(t)
            xt_hi(t)
            xt_lo(t)

        def g_make(e, *_):
            wt = xr[:, 6, :].rearrange("p (h n) -> p h n", h=4)
            for h in range(4):
                last = e.matmul(pz[0][:, 128 * h:128 * h + 128], wt[:, h, :], wt[:, h, :], start=True, stop=True)
            return last
        do("pe", g_make, [("whr", 0)], ("G", 0))
        g4 = [xreg[:, 4096 + 512 * i:4608 + 512 * i] for i in range(2)]
        high(("Ghi", 0), g4[0], pz[0], [("G", 0)])
        rest(("Glo", 0), g4[1], pz[0], g4[0], [("Ghi", 0)])
        wh_raw = xr[:, 7, :].rearrange("p (h n) -> p h n", h=4)
        high(("whhi", 0), whs[:, :, 0, :], wh_raw, [("whr2", 0)])
        rest(("whlo", 0), whs[:, :, 1, :], wh_raw, whs[:, :, 0, :], [("whhi", 0)])
        for h in range(2):
            ct_split(0, h, first=True)
            ct_split(0, h + 2)
        for k in range(4):
            high(("wghi", k), wgs[0][:, k, :], tmp[:, k, :], [("wgr", 0)])
            rest(("wglo", k), wgs[1][:, k, :], tmp[:, k, :], wgs[0][:, k, :], [("wghi", k)])
        norm(4)
        stats(5)
        rstd(5)


        for g in range(NG):
            n = 4 * g + 4
            more = g + 1 < NG
            late = g >= LATE
            if g == 0:
                for hp in range(2):
                    dma((f"ct{hp}", 1), raw[:, 2 * hp:2 * hp + 2, :], ct_v[:, 2 * hp:2 * hp + 2, 512:1024],
                        [("ctlf", (0, 1)) if hp == 0 else ("ctlo", (0, 3))])
            if g < 12:
                to_scratch(g)
            if 1 <= g <= 8:
                weight_load(g - 1)

            def dve_next(t):
                if t < 4 * NG:
                    stats(t)
                    rstd(t)

            if more:
                ct_split(g + 1, 0)
            z(g, 0)
            z(g, 1)
            for h in range(2):
                z_hi(g, h)
                z_lo(g, h)
            if more:
                norm(n + 1)
            for j in range(4):
                t = 4 * g + j
                if j == 1:
                    z(g, 2)
                    z(g, 3)
                    for h in (2, 3):
                        z_hi(g, h)
                        z_lo(g, h)
                if j == 3:
                    scores(g, 0)
                    scores(g, 1)
                v(t)
                v_out(t)
                if more:
                    xt(n + j)
                    xt_hi(n + j)
                    xt_lo(n + j)
                    if j == 0 or j == 1:
                        dve_next(n + j + 2)
                        norm(n + j + 2)
                    if j == 2:
                        dve_next(n + 4)
                    if j == 3:
                        if n + 4 < 4 * NG:
                            norm(n + 4)
                        dve_next(n + 5)
                if not late:
                    w(t)
                    w_out(t)
                if more and j < 3:
                    ct_split(g + 1, j + 1)
                if 2 <= g < 14 and j >= 2:
                    c = g - 2
                    if c >= 8:
                        low_load(c, j - 2)
                    low_bits(c, j - 2)
                q = 2 * g + 4 + j // 2
                if j % 2 == 1 and q < 2 * NG:
                    x_load(q)
                if g + 2 < NG and j % 2 == 1:
                    ct_load(g + 2, j // 2)
                v_store(t)
                if not late:
                    w_store(t)
            scores(g, 2)
            scores(g, 3)

        all_read = ("s", (NG - 1, 3))
        do("dve", lambda e: e.tensor_reduce(lowm[:, :], low[:, :], AX.X, ALU.max), [("low", 23)], ("lowm", 0))
        do("pe", lambda e, *_: e.matmul(ptb[0:1, 0, 0:1], lowm[:, :], ones[:, :], start=True, stop=True),
           [("lowm", 0), ("ones", 0), ("tbe", ("x", 63))], ("lows", 0))
        do("dve", lambda e: e.tensor_copy(flag[:, :], ptb[0:1, 0, 0:1]), [("lows", 0)], ("flag", 0))

        def v_load(p):
            after = [("vlo", p - 1)] if p else [("ctlo", (NG - 1, 3))]
            after += [("vst0", 2 * p), ("vst1", 2 * p + 1)]
            dma(("vld", p), raw[:, 0:2, :], v_s[:, 2 * p:2 * p + 2, :], after)

        def w_load(t):
            after = [("tb", ("wy", t - 2))] if t >= 2 else [("ctlo", (NG - 1, 3))]
            after.append((f"wst{t % 2}", t))
            dma((f"wl{t % 2}", t), raw[:, 2 + t % 2, :], w_s[:, t, :], after)

        def x_again(q):
            if q >= 4:
                after = [(f"out{q % 4}", q - 4)]
            elif q < 2:
                after = [("xn", 2 * q + 57)] + [("ad", 0)] * q
            else:
                after = [("wolo", 3), ("alo", 0)]
            dma((f"xa{q % 4}", q), xr[:, 2 * q % 8:2 * q % 8 + 2, :], x_v[:, 2 * q:2 * q + 2, :], after)

        dma(("dec", 0), xr[:, 3, :], decay, [("xn", 59)])
        v_load(0)
        w_load(0)
        wo_v = wo.rearrange("(k p) n -> p k n", p=128)
        dma(("wor", 0), xr[:, 4:7, :], wo_v[:, 0:3, :], [("xn", 62)])
        dma(("wor3", 0), stg[:, 0:512], wo_v[:, 3, :], [("low", 23)])
        x_again(0)
        w_load(1)
        x_again(1)

        a_t = xr[:, 7, :].rearrange("p (h n) -> p h n", h=4)
        dec_t = xr[:, 3, :].rearrange("p (h n) -> p h n", h=4)
        do("act", lambda e: e.copy(a_t, psc[:, :, 1, :]), [all_read, ("xn", 63)], ("a", "part"))
        do("dve", lambda e: e.tensor_tensor(a_t, psc[:, :, 0, :], a_t, ALU.add), [("a", "part")], ("as", 0))
        do("dve", lambda e: e.tensor_tensor(a_t, a_t, dec_t, ALU.mult), [("as", 0), ("dec", 0)], ("ad", 0))
        do("dve", lambda e: e.scalar_tensor_tensor(xr[:, 7, :], xr[:, 7, :], -1.0, xr[:, 7, :], ALU.mult, ALU.max),
           [("ad", 0)], ("ad", 1))
        do("dve", lambda e: e.tensor_scalar(xr[:, 7, :], xr[:, 7, :], 1.0, None, ALU.max), [("ad", 1)], ("ad", 2))
        high(("ahi", 0), xreg[:, 5632:6144], xr[:, 7, :], [("ad", 2), ("v", 63)])
        rest(("alo", 0), a_lo_t[:, :], xr[:, 7, :], xreg[:, 5632:6144], [("ahi", 0)])

        def v_hi(p):
            after = [("vld", p), all_read] + ([("o", p - 1)] if p else [])
            high(("vhi", p), vs[0], raw[:, 0:2, :], after)

        def v_lo(p):
            rest(("vlo", p), vs[1], raw[:, 0:2, :], vs[0], [("vhi", p)])

        v_hi(0)
        v_lo(0)
        for k in range(4):
            src = xr[:, 4 + k, :] if k < 3 else stg[:, 0:512]
            high(("wohi", k), wos[0][:, k, :], src, [("wor", 0) if k < 3 else ("wor3", 0), all_read])
            rest(("wolo", k), wos[1][:, k, :], src, wos[0][:, k, :], [("wohi", k)])
        do("act", lambda e: e.activation(tg[:, :], colsb[:, 2 * NI:2 * NI + 2], ACT.Tanh), [("cols", 0)], ("tg", 0))
        do("dve", lambda e: e.tensor_scalar(ds, ds, tg[:, 1:2], None, ALU.mult), [("rows", 0), ("tg", 0)], ("ds", 0))

        def o(q, p):
            after = [("vlo", p), ("alo", 0)] + ([("y1", 2 * p - 1)] if p else [])

            def make(e, *_):
                for h in range(4):
                    last = three(e, po[:, h // 2, :, 128 * (h % 2):128 * (h % 2) + 128], a_parts, vs, 0, 1,
                                 (slice(None), h, slice(None)), (slice(None), slice(None), slice(128 * h, 128 * h + 128)))
                return last
            do(q, make, after, ("o", p))

        yb_read = [("vst1", 63)]

        def halves(ap):
            return ap.rearrange("p (a n) -> p a n", a=2)

        def y_first(t):
            o_t = po[:, :, t % 2, :]
            do("dve", lambda e: e.bn_stats(st[:, t % 4, :], o_t), [("o", t // 2)], ("st", 64 + t))
            do("dve", lambda e: e.bn_aggr(mv[:, t % 8, :], st[:, t % 4, :]), [("st", 64 + t)], ("mv", 64 + t))
            power(("rs", 64 + t), rs[:, t % 8:t % 8 + 1], mv[:, t % 8, 1:2], 1e-3, [("mv", 64 + t)])
            do("dve", lambda e: e.scalar_tensor_tensor(halves(yb), o_t, mv[:, t % 8, 0:1], halves(gamma), ALU.subtract,
                                                       ALU.mult), [("mv", 64 + t), ("rows", 0), yb_read[0]], ("y1", t))
            yb_read[0] = ("wy", t)

        def y_second(t):
            do("dve", lambda e: e.scalar_tensor_tensor(yb, yb, rs[:, t % 8:t % 8 + 1], beta, ALU.mult, ALU.add),
               [("y1", t), ("rs", 64 + t)], ("y2", t))
            w_t = raw[:, 2 + t % 2, :]
            do("dve", lambda e: e.tensor_tensor(w_t, w_t, yb, ALU.mult), [("y2", t), (f"wl{t % 2}", t)], ("wy", t))

        def wy_t(q, t):
            transpose(q, ("wy", t), raw[:, 2 + t % 2, :], [("wy", t)])

        def wy_hi(t):
            transposed_hi(("wy", t), wyt[0][:, :, :], [("wo", t - 1)] if t else [])

        def wy_lo(t):
            transposed_lo(("wy", t), wyt[1][:, :, :], wyt[0][:, :, :])

        def wo_mm(q, t):
            after = [("tbe", ("wy", t)), ("wolo", 3), ("x1", t - 1) if t else ("wev", 4 * LATE - 1)]

            def make(e, *_):
                for k in range(4):
                    last = three(e, pyb[:, :], wyt, wos, k, 4, (slice(None), k, slice(None)),
                                 (slice(None), k, slice(None)))
                return last
            do(q, make, after, ("wo", t))

        def x1(t):
            x_t = xr[:, t % 8, :]
            do("dve", lambda e: e.scalar_tensor_tensor(x_t, pyb[:, :], tg[:, 0:1], x_t, ALU.mult, ALU.add),
               [("wo", t), (f"xa{t // 2 % 4}", t // 2), ("tg", 0)], ("x1", t))

        def stats2(t):
            do("dve", lambda e: e.bn_stats(st2[:, t % 4, :], xr[:, t % 8, :]), [("x1", t)], ("st2", t))
            do("dve", lambda e: e.bn_aggr(mv2[:, t % 8, :], st2[:, t % 4, :]), [("st2", t)], ("mv2", t))
            power(("rs2", t), rs2[:, t % 8:t % 8 + 1], mv2[:, t % 8, 1:2], 1e-5, [("mv2", t)])

        def norm2(t):
            after = [("rs2", t), ("mv2", t), ("x1", t)] + ([("tb", ("x2", t - 2))] if t >= 2 else [])
            do("dve", lambda e: e.tensor_scalar(xn[:, t % 2, :], xr[:, t % 8, :], mv2[:, t % 8, 0:1],
                                                rs2[:, t % 8:t % 8 + 1], ALU.subtract, ALU.mult), after, ("xn2", t))

        def x2_dst(t):
            return [p[:, :, 128 * (t % 4):128 * (t % 4) + 128] for p in x2t]

        def x2_t(q, t):
            transpose(q, ("x2", t), xn[:, t % 2, :], [("xn2", t)])

        def slot_free(n):
            g, j = divmod(n, 15)
            return ("h", 11 * g + j) if j < 11 else ("oe", 4 * g + j - 11)

        def product(e, exact, dst, lhs, rhs, k, n, left):
            act, wt = (rhs, lhs) if left else (lhs, rhs)
            if exact:
                pairs = [(wt, act[0]), (wt, act[1])]
            else:
                pairs = [(f(wt), f(act[0])), (wt, act[1])]
            for i, (a, b) in enumerate(pairs):
                p = (a, b) if left else (b, a)
                last = e.matmul(dst, p[0], p[1], start=(k == 0 and i == 0), stop=(k == n - 1 and i == 1))
            return last

        def up_mm(g, j):
            n, m = 15 * g + j, 11 * g + j
            for which, (wt, kind) in enumerate(((gate, "gm"), (up, "um"))):
                after = []
                if which == 0:
                    if j == 0:
                        after += [("tbe", ("x2", 4 * g + 3))]
                        if g == 0:
                            after += [(f"wld{c}", 0) for c in range(8)] + [("wev", 62), ("wev", 63), ("as", 0), ("flag", 0)]
                    if n >= 2:
                        after.append(slot_free(n - 2))

                def make(e, exact, which=which, wt=wt):
                    for k in range(4):
                        last = product(e, exact, banks[2 * (n % 2) + which], wt[:, k, 128 * j:128 * j + 128],
                                       [x2t[0][:, k, :], x2t[1][:, k, :]], k, 4, True)
                    return last
                do("pe2", make, after, (kind, m))

        def silu(g, j):
            m, n = 11 * g + j, 15 * g + j
            after = [("gm", m)]
            after += [("hlo", m - 3)] if m >= 3 else [("wst0", 62), ("wst1", 63)]
            do("act", lambda e: e.activation(tmp[:, m % 3, :], banks[2 * (n % 2)], ACT.Silu,
                                             scale=colsb[:, j:j + 1]), after, ("si", m))

        def hidden(g, j):
            m, n = 11 * g + j, 15 * g + j
            s_t = tmp[:, m % 3, :]
            do("dve", lambda e: e.scalar_tensor_tensor(s_t, banks[2 * (n % 2) + 1], colsb[:, NI + j:NI + j + 1], s_t,
                                                       ALU.mult, ALU.mult), [("si", m), ("um", m)], ("h", m))

        def hidden_hi(g, j):
            m = 11 * g + j
            high(("hhi", m), hid[0][:, j, :], tmp[:, m % 3, :], [("h", m)])

        def hidden_lo(g, j):
            m = 11 * g + j
            rest(("hlo", m), hid[1][:, j, :], tmp[:, m % 3, :], hid[0][:, j, :], [("hhi", m)])

        def down_mm(g, t):
            n = 15 * g + 11 + t
            sl = slice(128 * t, 128 * t + 128)

            def make(e, exact, lo=0, hi=NI):
                for i in range(lo, hi):
                    last = product(e, exact, banks[2 * (n % 2)], [hid[0][:, i, sl], hid[1][:, i, sl]],
                                   down[:, i, :], i, NI, False)
                return last
            after = [slot_free(n - 2), ("hlo", 11 * g + 9)] + ([("dld", 0)] if g == 0 else [])
            do("pe2", lambda e, exact: make(e, exact, 0, NI - 1), after)
            do("pe2", lambda e, exact: make(e, exact, NI - 1, NI), [("hlo", 11 * g + 10)], ("dn", 4 * g + t))

        def finish(t):
            g, j = divmod(t, 4)
            n = 15 * g + 11 + j
            do("dve", lambda e: e.tensor_tensor(yb, banks[2 * (n % 2)], ds, ALU.mult),
               [("dn", t), ("ds", 0), yb_read[0]], ("oe", t))
            yb_read[0] = ("of", t)
            do("dve", lambda e: e.tensor_tensor(xr[:, t % 8, :], xr[:, t % 8, :], yb, ALU.add), [("oe", t), ("xn2", t)],
               ("of", t))

        def out_store(q):
            dma((f"out{q % 4}", q), out_v[:, 2 * q:2 * q + 2, :], xr[:, 2 * q % 8:2 * q % 8 + 2, :], [("of", 2 * q + 1)])

        def att_pe(q, g, s):
            a, p = 4 * g, 2 * g
            for step, make in ((0, lambda: o(q, p)), (2, lambda: wy_t(q, a)), (3, lambda: wo_mm(q, a)),
                               (3, lambda: wy_t(q, a + 1)), (4, lambda: wo_mm(q, a + 1)), (5, lambda: o(q, p + 1)),
                               (7, lambda: wy_t(q, a + 2)), (8, lambda: wo_mm(q, a + 2)), (8, lambda: wy_t(q, a + 3)),
                               (9, lambda: wo_mm(q, a + 3)), (11, lambda: x2_t(q, a)), (12, lambda: x2_t(q, a + 1)),
                               (13, lambda: x2_t(q, a + 2)), (14, lambda: x2_t(q, a + 3))):
                if step == s:
                    make()

        def att_act(g, s):
            a, p = 4 * g, 2 * g
            if s in (2, 3, 7, 8):
                wy_hi(a + {2: 0, 3: 1, 7: 2, 8: 3}[s])
            if s == 4:
                v_hi(p + 1)
            if s == 11 and g + 1 < NG:
                v_hi(p + 2)
            if s >= 11:
                t = a + s - 11
                transposed_hi(("x2", t), x2_dst(t)[0])

        def att_dve(g, s, end):
            a, p = 4 * g, 2 * g
            if not end:
                if s in (2, 3, 7, 8):
                    wy_lo(a + {2: 0, 3: 1, 7: 2, 8: 3}[s])
                if s >= 11:
                    t = a + s - 11
                    transposed_lo(("x2", t), x2_dst(t)[1], x2_dst(t)[0])
                return
            if s in (1, 2, 6, 7):
                y_second(a + {1: 0, 2: 1, 6: 2, 7: 3}[s])
            if s in (0, 1, 5, 6):
                y_first(a + {0: 0, 1: 1, 5: 2, 6: 3}[s])
            if s in (3, 4, 8, 9):
                x1(a + {3: 0, 4: 1, 8: 2, 9: 3}[s])
                stats2(a + {3: 0, 4: 1, 8: 2, 9: 3}[s])
            if s == 4:
                v_lo(p + 1)
            if s == 11 and g + 1 < NG:
                v_lo(p + 2)
            if 9 <= s <= 12:
                norm2(a + s - 9)

        def att_sp(g, s):
            a, p = 4 * g, 2 * g
            if s == 1 and g:
                x_again(2 * g)
            if s == 2:
                v_load(p + 1)
            if s == 3:
                w_load(a + 2)
            if s == 4:
                w_load(a + 3)
                if g:
                    x_again(2 * g + 1)
            if s == 6 and g + 1 < NG:
                v_load(p + 2)
            if s == 8 and g + 1 < NG:
                w_load(a + 4)
            if s == 9 and g + 1 < NG:
                w_load(a + 5)

        left = list(range(4 * LATE, 4 * NG))
        for t in (left.pop(0), left.pop(0)):
            w(t)
            w_out(t)
            w_store(t)
        for s in range(15):
            att_pe("pe", 0, s)
            att_act(0, s)
            att_dve(0, s, False)
            att_dve(0, s, True)
            att_sp(0, s)
            if left and s in (0, 1, 2, 3, 5, 7):
                t = left.pop(0)
                w(t)
                w_out(t)
                w_store(t)
            if s == 7:
                dma(("dld", 0), f(down), down_s.rearrange("(i p) n -> p i n", p=128),
                    [(f"scr{c}", 0) for c in range(8, 12)] + [("w", 63), ("Glo", 0)])
        assert not left

        for g in range(NG):
            nxt = g + 1 < NG
            for s in range(15):
                if nxt:
                    att_pe("pe2", g + 1, s)
                if s < 11:
                    up_mm(g, s)
                else:
                    down_mm(g, s - 11)
                if nxt:
                    att_act(g + 1, s)
                if 1 <= s <= 11:
                    hidden(g, s - 1)
                    hidden_hi(g, s - 1)
                if s < 11:
                    silu(g, s)
                if nxt:
                    att_dve(g + 1, s, False)
                if 1 <= s <= 11:
                    hidden_lo(g, s - 1)
                if s == 0 and g:
                    finish(4 * g - 1)
                    out_store(2 * g - 1)
                if s >= 12:
                    finish(4 * g + s - 12)
                if nxt:
                    att_dve(g + 1, s, True)
                    att_sp(g + 1, s)
                if s == 13:
                    out_store(2 * g)
        finish(4 * NG - 1)
        out_store(2 * NG - 1)
        do("sp", lambda e: None, [(f"out{q % 4}", q) for q in range(2 * NG - 4, 2 * NG)])

        sems = {kind: stack.enter_context(nc.semaphore(f"s_{kind}")) for kind in plan.total}
        block = stack.enter_context(nc.Block())

        @block.sync
        def _(e):
            plan.emit("sp", e, sems, {})

        @block.scalar
        def _(e):
            plan.emit("act", e, sems, {})

        @block.vector
        def _(e):
            plan.emit("dve", e, sems, {})

        @block.gpsimd
        def _(e):
            plan.emit("pool", e, sems, {})

        @block.tensor
        def _(e):
            seen = {}
            plan.emit("pe", e, sems, seen)
            e.wait_ge(sems["flag"], plan.value[("flag", 0)])
            some_low = e.alloc_register("some_low")
            e.reg_load(some_low, flag[0:1, 0:1])
            with e.If_eq(some_low, 0):
                plan.emit("pe2", e, sems, dict(seen), True)
            with e.Else():
                plan.emit("pe2", e, sems, dict(seen), False)


def decay_t():
    gam = np.float32(1.0) - np.float32(2.0) ** (-5.0 - np.arange(H, dtype=np.float32))
    idx = np.arange(S, dtype=np.float32)
    expo = idx[None, :] - idx[:, None]
    m = np.where(expo[None] <= 0, gam[:, None, None].astype(np.float64) ** np.minimum(expo, 0)[None], 0.0)
    m = m / np.sqrt(m.sum(axis=-1))[:, None, :] / np.sqrt(float(HD))
    return np.ascontiguousarray(m.transpose(2, 0, 1).reshape(S, H * S).astype(np.float32))


def kernel(x, ctx_2048, g_xattn, g_ffn, L0_xattn_Wh, L0_xattn_wg_w, L0_xattn_wo_w, L0_xattn_gn_gamma, L0_xattn_gn_beta,
           L0_ffn_gate_w, L0_ffn_up_w, L0_ffn_down_w, L0_ffn_gate_s, L0_ffn_up_s, L0_ffn_down_s):
    import numpy as _np
    import concourse.bacc as _bacc
    from concourse import mybir as _mybir
    from concourse.bass_utils import run_bass_kernel_spmd as _run

    def laid(a):
        return _np.ascontiguousarray(a)

    c = {k: _np.asarray(v) for k, v in dict(
        x=x, ctx=ctx_2048, gx=g_xattn, gf=g_ffn, wh=L0_xattn_Wh, wg=L0_xattn_wg_w, wo=L0_xattn_wo_w,
        gamma=L0_xattn_gn_gamma, beta=L0_xattn_gn_beta, gw=L0_ffn_gate_w, uw=L0_ffn_up_w, dw=L0_ffn_down_w,
        gs=L0_ffn_gate_s, us=L0_ffn_up_s, ds=L0_ffn_down_s).items()}
    arrays = {
        "in_x": laid(c["x"]),
        "in_ctx_t": laid(c["ctx"].transpose(2, 0, 1).reshape(D, B * S)),
        "in_wh": laid(c["wh"]),
        "in_wh_t": laid(c["wh"].transpose(0, 2, 1)),
        "in_wg": laid(c["wg"]),
        "in_wo": laid(c["wo"]),
        "in_gate_t": laid(c["gw"].T),
        "in_up_t": laid(c["uw"].T),
        "in_down_t": laid(c["dw"].T),
        "in_cols": laid(_np.concatenate([c["gs"].reshape(NI, 128).T, c["us"].reshape(NI, 128).T,
                                         _np.broadcast_to(c["gx"][0:1], (128, 1)),
                                         _np.broadcast_to(c["gf"][0:1], (128, 1))], axis=1)),
        "in_rows": laid(_np.broadcast_to(_np.stack([c["gamma"], c["beta"], c["ds"]]), (128, 3, D))),
        "in_decay": decay_t(),
        "in_eye": _np.eye(128, dtype=_np.float32),
    }
    nc = _bacc.Bacc("TRN2", target_bir_lowering=False, num_devices=1)
    args = [nc.dram_tensor(n, a.shape, _mybir.dt.from_np(a.dtype), kind="ExternalInput").ap() for n, a in arrays.items()]
    args.append(nc.dram_tensor("out", (B, S, D), _mybir.dt.float32, kind="ExternalOutput").ap())
    gated_layer(nc, *args)
    r = _run(nc, [arrays], core_ids=[0])
    return r.results[0]["out"]
```

```python
import numpy as np
import concourse.bass as bass
from concourse import mybir
from contextlib import ExitStack

B, S, D, H, HD, NI = 64, 128, 512, 4, 128, 11
INTER = NI * 128
NG = B // 4
LATE = B - 4


class Plan:

    def __init__(self):
        self.queue, self.total, self.value = {}, {}, {}

    def do(self, engine, make, after=(), then=None, inc=1):
        if then is not None:
            kind = then[0]
            self.total[kind] = self.total.get(kind, 0) + inc
            assert then not in self.value
            self.value[then] = self.total[kind]
        self.queue.setdefault(engine, []).append((tuple(after), make, then, inc))

    def emit(self, name, engine, sems, seen, *args):
        for after, make, then, inc in self.queue.get(name, ()):
            for event in after:
                value = self.value[event]
                if seen.get(event[0], 0) < value:
                    seen[event[0]] = value
                    engine.wait_ge(sems[event[0]], value)
            made = make(engine, *args)
            if then is not None:
                made.then_inc(sems[then[0]], inc)


def gated_layer(nc, x, ctx_t, wh, wh_t, wg, wo, gate_t, up_t, down_t, cols, rows, decay, eye, out):
    f32, f32r, u32, i32 = mybir.dt.float32, mybir.dt.float32r, mybir.dt.uint32, mybir.dt.int32
    ALU = mybir.AluOpType
    ACT = mybir.ActivationFunctionType
    AX = mybir.AxisListType

    stack = ExitStack()
    with stack:
        def sb(name, shape, dt=f32):
            return stack.enter_context(nc.sbuf_tensor(name, shape, dt))

        gate = sb("gate", [128, 4, INTER], f32r)
        up = sb("up", [128, 4, INTER], f32r)
        xreg = sb("xreg", [128, 12 * 512], f32r)
        wgs = [xreg[:, 2048 * i:2048 * i + 2048].rearrange("p (k n) -> p k n", k=4) for i in range(2)]
        gs_ = [xreg[:, 4096 + 512 * i:4608 + 512 * i].rearrange("p (h n) -> p h n", h=4) for i in range(2)]
        whs = xreg[:, 5120:6144].rearrange("p (h q n) -> p h q n", h=4, q=2)
        down = xreg[:, 0:NI * 512].rearrange("p (i n) -> p i n", i=NI)
        a_sb = [sb(f"a{i}", [128, 512], f32r) for i in range(2)]
        a_parts = [a[:, :].rearrange("p (h n) -> p h n", h=4) for a in a_sb]
        reg = sb("reg", [128, 84 * 256], f32r)

        def part(kib, n, **dims):
            v = reg[:, 256 * kib:256 * kib + n * int(np.prod(list(dims.values())))]
            names = list(dims)
            return v.rearrange(f"p ({' '.join(names)} n) -> p {' '.join(names)} n", **dims)

        xnt = [[part(16 * b + 8 * i, 512, k=4) for i in range(2)] for b in range(2)]
        zt = part(32, 512, q=2, h=4)
        ct = [[part(48 + 20 * b + 8 * i, 512, h=4) for i in range(2)] for b in range(2)]
        hid = [part(22 * i, 512, i=NI) for i in range(2)]
        vs = [part(48 + 4 * i, 512, b=2) for i in range(2)]
        x2t = [part(68 + 8 * i, 512, k=4) for i in range(2)]
        wos = [[reg[:, 256 * kib:256 * kib + 512] for kib in kibs]
               for kibs in ((56, 58, 60, 62), (64, 66, 44, 46))]
        wyt = [sb(f"wyt{i}", [128, 4, 128], f32r) for i in range(2)]
        vs_first = [part(4 + 4 * i, 512, b=2) for i in range(2)]
        wyt_first = [part(2 * i, 128, k=4) for i in range(2)]

        xr = sb("xr", [128, 8, 512])
        xn = sb("xn", [128, 2, 512])
        tmp = sb("tmp", [128, 4, 512])
        raw = sb("raw", [128, 4, 512])
        stg = sb("stg", [128, 704])
        colsb = sb("colsb", [128, 2 * NI + 2])
        rowsb = sb("rowsb", [128, 3, 512])
        ident = sb("ident", [128, 128])
        tg = sb("tg", [128, 2])
        st = sb("st", [128, 4, 6])
        mv = sb("mv", [128, 8, 2])
        rs = sb("rs", [128, 8])
        st2 = sb("st2", [128, 4, 6])
        mv2 = sb("mv2", [128, 8, 2])
        rs2 = sb("rs2", [128, 8])
        low = sb("low", [128, 24])
        lowm = sb("lowm", [128, 1])
        ones = sb("ones", [128, 1])
        nhalf = sb("nhalf", [128, 1])
        flag = sb("flag", [1, 1], i32)
        gamma, beta, ds = rowsb[:, 0, :], rowsb[:, 1, :], rowsb[:, 2, :]
        yb = tmp[:, 3, :]

        ps = [stack.enter_context(nc.psum_tensor(f"ps{i}", [128, 4, 2, 128], f32)) for i in range(2)]
        pv, psc = ps
        banks = [p[:, 2 * i:2 * i + 2, :, :].rearrange("p a b n -> p (a b n)") for p in ps for i in range(2)]
        po = stack.enter_context(nc.psum_tensor("po", [128, 2, 2, 256], f32))
        ptb = stack.enter_context(nc.psum_tensor("ptb", [128, 4, 128], f32))
        pyb = stack.enter_context(nc.psum_tensor("pyb", [128, 512], f32))
        pz = [po[:, i, :, :].rearrange("p a n -> p (a n)") for i in range(2)]

        v_s = nc.dram_tensor("v_scratch", [128, B, D], f32, kind="Internal").ap()
        w_s = nc.dram_tensor("w_scratch", [128, B, D], f32, kind="Internal").ap()
        gate_s = nc.dram_tensor("gate_scratch", [D, INTER], f32, kind="Internal").ap()
        up_s = nc.dram_tensor("up_scratch", [D, INTER], f32, kind="Internal").ap()
        down_s = nc.dram_tensor("down_scratch", [INTER, D], f32, kind="Internal").ap()

        x_v = x.rearrange("b s d -> s b d")
        out_v = out.rearrange("b s d -> s b d")
        ct_v = ctx_t.rearrange("(h p) n -> p h n", p=128)
        down_flat = down_t.rearrange("(p a) n -> p (a n)", p=128)

        plan = Plan()
        do = plan.do

        def f(ap):
            return ap.bitcast(f32)

        def dma(key, dst, src, after=()):
            do("sp", lambda e: e.dma_start(dst, src), after, key, 16)

        def high(key, dst, src, after):
            do("act", lambda e: e.copy(dst, src), after, key)

        def rest(key, dst, src, hi, after):
            do("dve", lambda e: e.tensor_tensor(dst, src, f(hi), ALU.subtract), after, key)

        def three(e, dst, lhs, rhs, k, n):
            for i, (a, b) in enumerate(((0, 0), (0, 1), (1, 0))):
                last = e.matmul(dst, lhs[a], rhs[b], start=(k == 0 and i == 0), stop=(k == n - 1 and i == 2))
            return last

        def x_load(q):
            after = [("xn", 2 * q - 7)] if q >= 4 else []
            if q == 3:
                after = [("whlo", 0), ("G", 0)]
            dma((f"xl{q % 4}", q), xr[:, 2 * q % 8:2 * q % 8 + 2, :], x_v[:, 2 * q:2 * q + 2, :], after)

        def stats(t):
            do("dve", lambda e: e.bn_stats(st[:, t % 4, :], xr[:, t % 8, :]), 
               [(f"xl{t // 2 % 4}", t // 2) if t else ("xf", 0)], ("st", t))
            do("dve", lambda e: e.bn_aggr(mv[:, t % 8, :], st[:, t % 4, :]), [("st", t)], ("mv", t))

        def power(key, dst, var, eps, after):
            do("pool", lambda e: e.tensor_scalar(dst, var, eps, None, ALU.add), after, ("eps", key))
            do("pool", lambda e: e.tensor_tensor(dst, dst, nhalf[:, :], ALU.pow), [("eps", key), ("ones", 1)], key)

        def rstd(t):
            power(("rs", t), rs[:, t % 8:t % 8 + 1], mv[:, t % 8, 1:2], 1e-5, [("mv", t)])

        def norm(t):
            after = [("rs", t), ("mv", t)] + ([("tb", ("x", t - 2))] if t >= 2 else [])
            do("dve", lambda e: e.tensor_scalar(xn[:, t % 2, :], xr[:, t % 8, :], mv[:, t % 8, 0:1],
                                                rs[:, t % 8:t % 8 + 1], ALU.subtract, ALU.mult), after, ("xn", t))

        tb_last = {}

        tb_banks = [ptb[:, :, :], pyb[:, :].rearrange("p (k n) -> p k n", k=4)]
        tb_banks += [p[:, 2 * i:2 * i + 2, :, :].rearrange("p a b n -> p (a b) n") for p in (psc, pv) for i in range(2)]
        tb_elsewhere = {("x", 1): 2, ("x", 2): 3, ("x", 3): 1, ("wy", 1): 5, ("wy", 3): 5, ("x2", 1): 5, ("x2", 3): 5}

        def tb_of(key):
            return tb_banks[tb_elsewhere.get(key, 0)]

        def transpose(q, key, src, after):
            bank, place = tb_of(key), tb_elsewhere.get(key, 0)
            if tb_last.get(place):
                after = [*after, ("tbe", tb_last[place])]
            tb_last[place] = key

            def make(e, *_):
                for k in range(4):
                    last = e.transpose(bank[:, k, :], src[:, 128 * k:128 * k + 128], ident[:, :])
                return last
            do(q, make, after, ("tb", key))

        def transposed_hi(key, dst, after=()):
            high(("tbh", key), dst, tb_of(key), [("tb", key), *after])

        def transposed_lo(key, dst, hi):
            rest(("tbe", key), dst, tb_of(key), hi, [("tbh", key)])

        def xt_dst(t):
            return [p[:, :, 128 * (t % 4):128 * (t % 4) + 128] for p in xnt[t // 4 % 2]]

        def xt(t):
            transpose("pe", ("x", t), xn[:, t % 2, :], [("xn", t), ("c", "eye")])

        def xt_hi(t):
            transposed_hi(("x", t), xt_dst(t)[0])

        def xt_lo(t):
            transposed_lo(("x", t), xt_dst(t)[1], xt_dst(t)[0])

        def z(g, h):
            after = [("tbe", ("x", 4 * g + 3)), ("Glo", 0)]
            n = 4 * g + h
            if n >= 2:
                after.append(("zlo", n - 2))
            do("pe", lambda e, *_: three(e, pz[h % 2], [p[:, h, :] for p in gs_], [p[:, h, :] for p in xnt[g % 2]], 0, 1), after, ("z", n))

        def z_hi(g, h):
            high(("zhi", 4 * g + h), zt[:, 0, h, :], pz[h % 2], [("z", 4 * g + h)])

        def z_lo(g, h):
            rest(("zlo", 4 * g + h), zt[:, 1, h, :], pz[h % 2], zt[:, 0, h, :], [("zhi", 4 * g + h)])

        def ct_load(g, hp):
            after = [("ctlo", (g - 1, 2 * hp + 1))] if g else []
            dma((f"ct{hp}", g), raw[:, 2 * hp:2 * hp + 2, :], ct_v[:, 2 * hp:2 * hp + 2, 512 * g:512 * g + 512], after)

        def ct_split(g, h, first=False):
            a, b = ct[g % 2][0][:, h, :], ct[g % 2][1][:, h, :]
            after = [(f"ct{h // 2}", g)] + ([("s", (g - 2, 3))] if g >= 2 else [])
            do("act" if first else "pool", lambda e: (e.copy if first else e.tensor_copy)(a, raw[:, h, :]),
               after, ("cthf" if first else "cthi", (g, h)))
            do("dve" if first else "pool", lambda e: e.tensor_tensor(b, raw[:, h, :], f(a), ALU.subtract),
               [("cthf" if first else "cthi", (g, h))], ("ctlo", (g, h)) if not first else ("ctlf", (g, h)))

        def ct_ready(g):
            return [("ctlo", (g, 3))] + ([("ctlf", (0, 1))] if g == 0 else [])

        def v(t):
            g, b = divmod(t, 4)
            after = ct_ready(g) + [("whlo", 0)] + ([("vev", t - 1)] if t else [])

            def make(e, *_):
                for h in range(4):
                    for i in range(2):
                        last = e.matmul(pv[:, h, :, :], ct[g % 2][i][:, h, 128 * b:128 * b + 128], whs[:, h, :, :],
                                        start=(i == 0), stop=(i == 1))
                return last
            do("pe", make, after, ("v", t))

        def v_out(t):
            dst = tmp[:, 2 + t % 2, :].rearrange("p (h n) -> p h n", h=4)
            after = [("v", t)] + ([(f"vst{t % 2}", t - 2)] if t >= 2 else [("wglo", 2 + t)])
            do("act", lambda e: e.copy(dst, pv[:, :, 1, :]), after, ("vlow", t))
            do("dve", lambda e: e.tensor_tensor(dst, pv[:, :, 0, :], dst, ALU.add), [("vlow", t)], ("vev", t))

        def v_store(t):
            dma((f"vst{t % 2}", t), v_s[:, t, :], tmp[:, 2 + t % 2, :], [("vev", t)])

        def pw(t):
            return pyb[:, :] if t < LATE else banks[2 + t % 2]

        def w(t):
            after = [("tbe", ("x", t)), ("wglo", 3 if t else 0)] + ([("wev", t - (2 if t >= LATE else 1))] if t else [])
            if t >= LATE:
                after.append(("as", 0))

            def make(e, ks):
                sl = slice(128 * (t % 4), 128 * (t % 4) + 128)
                for k in ks:
                    last = three(e, pw(t), [p[:, k, sl] for p in xnt[t // 4 % 2]], [p[:, k, :] for p in wgs], k, 4)
                return last
            if t:
                do("pe", lambda e, *_: make(e, range(4)), after, ("w", t))
                return
            for k in range(4):
                do("pe", lambda e, *_, k=k: make(e, (k,)), after if k == 0 else [("wglo", k)], ("w", t) if k == 3 else None)

        def w_out(t):
            after = [("w", t)] + ([(f"wst{t % 2}", t - 2)] if t >= 2 else [("wglo", t)])
            do("act", lambda e: e.activation(tmp[:, t % 2, :], pw(t), ACT.Relu), after, ("wev", t))

        def w_store(t):
            dma((f"wst{t % 2}", t), w_s[:, t, :], tmp[:, t % 2, :], [("wev", t)])

        def scores(g, h):
            def make(e, *_):
                for b in range(4):
                    sl = slice(128 * b, 128 * b + 128)
                    for i in range(2):
                        last = e.matmul(psc[:, h, :, :], ct[g % 2][i][:, h, sl], zt[:, :, h, sl],
                                        start=(g == 0 and h % 2 == 0 and b == 0 and i == 0),
                                        stop=(g == NG - 1 and h % 2 == 1 and b == 3 and i == 1), skip_group_check=True)
                return last
            do("pe", make, [("zlo", 4 * g + h), *ct_ready(g)], ("s", (g, h)))

        chunks = ([(gate_t[128 * k:128 * k + 128, :], gate_s[128 * k:128 * k + 128, :], gate[:, k, :]) for k in range(4)]
                  + [(up_t[128 * k:128 * k + 128, :], up_s[128 * k:128 * k + 128, :], up[:, k, :]) for k in range(4)]
                  + [(down_t[352 * k:352 * k + 352, :], down_s[352 * k:352 * k + 352, :], None) for k in range(4)])

        def to_scratch(c):
            src, dst, _ = chunks[c]
            dma((f"scr{c}", 0), dst, src)

        def weight_load(c):
            _, src, dst = chunks[c]
            dma((f"wld{c}", 0), f(dst), src, [(f"scr{c}", 0)])

        def low_load(c, half):
            at = 1408 * (c - 8) + 704 * half
            after = [("low", 2 * c + half - 1)]
            dma(("lowld", 2 * c + half), stg[:, :], down_flat[:, at:at + 704], after)

        def low_bits(c, half):
            n = 2 * c + half
            if c < 8:
                src, after = chunks[c][2][:, 704 * half:704 * half + 704].bitcast(u32), [(f"wld{c}", 0)]
            else:
                src, after = stg[:, :].bitcast(u32), [("lowld", n)]
            do("dve", lambda e: e.tensor_scalar(stg[:, :].bitcast(u32), src, 0xFFF, None, ALU.bitwise_and), after,
               ("and", n))
            do("dve", lambda e: e.tensor_reduce(low[:, n:n + 1], stg[:, :].bitcast(i32), AX.X, ALU.max),
               [("and", n)], ("low", n))

        dma(("xf", 0), xr[:, 0, :], x_v[:, 0, :])
        dma(("c", "eye"), ident[:, :], eye)
        dma(("xl0", 0), xr[:, 1, :], x_v[:, 1, :])
        dma(("whr", 0), xr[:, 6, :].rearrange("p (h n) -> p h n", h=4), wh_t.rearrange("h e d -> e h d"))
        x_load(1)
        ct_load(0, 1)
        dma(("whr2", 0), xr[:, 7, :].rearrange("p (h n) -> p h n", h=4), wh.rearrange("h d e -> d h e"))
        ct_load(0, 0)
        x_load(2)
        dma(("wgr", 0), tmp[:, :, :], wg.rearrange("(k p) n -> p k n", p=128))
        x_load(3)
        dma(("cols", 0), colsb[:, :], cols)
        dma(("rows", 0), rowsb[:, :, :], rows)

        do("pool", lambda e: e.memset(ones[:, :], 1.0), (), ("ones", 0))
        do("pool", lambda e: e.memset(nhalf[:, :], -0.5), (), ("ones", 1))

        def g_make(e, *_):
            wt = xr[:, 6, :].rearrange("p (h n) -> p h n", h=4)
            for h in range(4):
                last = e.matmul(pz[0][:, 128 * h:128 * h + 128], wt[:, h, :], wt[:, h, :], start=True, stop=True)
            return last
        g4 = [xreg[:, 4096 + 512 * i:4608 + 512 * i] for i in range(2)]
        wh_raw = xr[:, 7, :].rearrange("p (h n) -> p h n", h=4)
        stats(0)
        rstd(0)
        stats(1)
        rstd(1)
        norm(0)
        xt(0)
        xt_hi(0)
        stats(2)
        rstd(2)
        do("pe", g_make, [("whr", 0)], ("G", 0))
        norm(1)
        xt(1)
        xt_hi(1)
        stats(3)
        rstd(3)
        high(("Ghi", 0), g4[0], pz[0], [("G", 0)])
        xt_lo(0)
        norm(2)
        xt(2)
        xt_hi(2)
        xt_lo(1)
        norm(3)
        xt(3)
        xt_hi(3)
        rest(("Glo", 0), g4[1], pz[0], g4[0], [("Ghi", 0)])
        xt_lo(2)
        xt_lo(3)
        high(("whhi", 0), whs[:, :, 0, :], wh_raw, [("whr2", 0)])
        rest(("whlo", 0), whs[:, :, 1, :], wh_raw, whs[:, :, 0, :], [("whhi", 0)])
        for h in range(2):
            ct_split(0, h, first=True)
            ct_split(0, h + 2)

        def wg_split(k):
            high(("wghi", k), wgs[0][:, k, :], tmp[:, k, :], [("wgr", 0)])
            rest(("wglo", k), wgs[1][:, k, :], tmp[:, k, :], wgs[0][:, k, :], [("wghi", k)])
        stats(4)
        rstd(4)


        all_read = ("s", (NG - 1, 3))

        def v_load(p):
            after = [("vlo", p - 1)] if p else [("ctlo", (NG - 1, 3))]
            after += [("vst0", 2 * p), ("vst1", 2 * p + 1)]
            dma(("vld", p), raw[:, 0:2, :], v_s[:, 2 * p:2 * p + 2, :], after)

        def w_load(t):
            after = [("tb", ("wy", t - 2))] if t >= 2 else [("ctlo", (NG - 1, 3))]
            after.append((f"wst{t % 2}", t))
            dma((f"wl{t % 2}", t), raw[:, 2 + t % 2, :], w_s[:, t, :], after)

        def x_again(q):
            if q >= 4:
                after = [(f"out{q % 4}", q - 4)]
            elif q < 2:
                after = [("xn", 2 * q + 57)] + [("ad", 0)] * q
            else:
                after = [("wolo", 3), ("alo", 0)]
            dma((f"xa{q % 4}", q), xr[:, 2 * q % 8:2 * q % 8 + 2, :], x_v[:, 2 * q:2 * q + 2, :], after)

        def vs_of(p):
            return vs_first if p == 1 else vs

        def wyt_of(t):
            return wyt_first if t in (1, 3) else wyt

        def py(t):
            return banks[0] if t in (1, 3) else pyb[:, :]

        def v_hi(p):
            after = [("vld", p), ("s", (NG - 2, 3)) if p == 0 else ("w", LATE - 1) if p == 1 else ("o", p - 1 if p > 2 else 0)]
            high(("vhi", p), vs_of(p)[0], raw[:, 0:2, :], after)

        def v_lo(p):
            rest(("vlo", p), vs_of(p)[1], raw[:, 0:2, :], vs_of(p)[0], [("vhi", p)])

        def wo_hi(k):
            src = xr[:, 4 + k, :] if k < 3 else stg[:, 0:512]
            high(("wohi", k), wos[0][k], src, [("wor", 0) if k < 3 else ("wor3", 0), ("s", (NG - 2, 3))])

        def wo_lo(k):
            src = xr[:, 4 + k, :] if k < 3 else stg[:, 0:512]
            rest(("wolo", k), wos[1][k], src, wos[0][k], [("wohi", k)] + ([all_read] if k > 1 else []))

        for g in range(NG):
            n = 4 * g + 4
            more = g + 1 < NG
            if g == 0:
                for hp in range(2):
                    dma((f"ct{hp}", 1), raw[:, 2 * hp:2 * hp + 2, :], ct_v[:, 2 * hp:2 * hp + 2, 512:1024],
                        [("ctlf", (0, 1)) if hp == 0 else ("ctlo", (0, 3))])
            if g < 12:
                to_scratch(g)
            if 1 <= g <= 8:
                weight_load(g - 1)

            def z_pair(g, h):
                z(g, h)
                z(g, h + 1)
                for i in (h, h + 1):
                    z_hi(g, i)
                    z_lo(g, i)

            def v_all(t):
                v(t)
                v_out(t)
                v_store(t)

            def w_all(t):
                w(t)
                w_out(t)
                w_store(t)

            def dve_next(t):
                if t < 4 * NG:
                    stats(t)
                    rstd(t)

            if more and g:
                ct_split(g + 1, 0)
            z_pair(g, 0)
            if g == 0:
                norm(4)
                for k in range(4):
                    wg_split(k)
                stats(5)
                rstd(5)
                ct_split(1, 0)
            if more:
                norm(n + 1)
            if not more:
                v_load(0)
                v_all(4 * g)
                dma(("wor", 0), xr[:, 4:7, :], wo.rearrange("(k p) n -> p k n", p=128)[:, 0:3, :], [("xn", 62)])
                z_pair(g, 2)
                v_all(4 * g + 1)
                w_load(0)
                w_load(1)
                x_again(0)
                scores(g, 0)
                v_all(4 * g + 2)
                scores(g, 1)
                v_hi(0)
                v_lo(0)
                v_load(1)
                for k in range(4):
                    wo_hi(k)
                wo_lo(0)
                wo_lo(1)
                scores(g, 2)
                scores(g, 3)
                w(LATE - 1)
                v(B - 1)
                break
            for j in range(4):
                t = 4 * g + j
                if j == 1:
                    z_pair(g, 2)
                if j == 3:
                    scores(g, 0)
                    scores(g, 1)
                v(t)
                v_out(t)
                xt(n + j)
                xt_hi(n + j)
                xt_lo(n + j)
                if j == 0 or j == 1:
                    dve_next(n + j + 2)
                    norm(n + j + 2)
                if j == 2:
                    dve_next(n + 4)
                if j == 3:
                    if n + 4 < B:
                        norm(n + 4)
                    dve_next(n + 5)
                if t < LATE - 1:
                    w(t)
                    w_out(t)
                if j < 3:
                    ct_split(g + 1, j + 1)
                if 2 <= g < 14 and j >= 2:
                    c = g - 2
                    if c >= 8:
                        low_load(c, j - 2)
                    low_bits(c, j - 2)
                if t == 4 * 14 + 1:
                    do("dve", lambda e: e.tensor_reduce(lowm[:, :], low[:, :], AX.X, ALU.max), [("low", 23)], ("lowm", 0))
                q = 2 * g + 4 + j // 2
                if j % 2 == 1 and q < 2 * NG:
                    x_load(q)
                if g + 2 < NG and j % 2 == 1:
                    ct_load(g + 2, j // 2)
                v_store(t)
                if t < LATE - 1:
                    w_store(t)
                if t == B - 5:
                    dma(("dec", 0), xr[:, 3, :], decay, [("xn", 59)])
                    dma(("wor3", 0), stg[:, 0:512], wo.rearrange("(k p) n -> p k n", p=128)[:, 3, :], [("low", 23)])
            scores(g, 2)
            scores(g, 3)

        do("pe", lambda e, *_: e.matmul(ptb[0:1, 0, 0:1], lowm[:, :], ones[:, :], start=True, stop=True),
           [("lowm", 0), ("ones", 0), ("tbe", ("x", 63))], ("lows", 0))
        a_t = xr[:, 7, :].rearrange("p (h n) -> p h n", h=4)
        dec_t = xr[:, 3, :].rearrange("p (h n) -> p h n", h=4)
        do("act", lambda e: e.copy(a_t, psc[:, :, 1, :]), [all_read, ("xn", 63)], ("a", "part"))
        w_out(LATE - 1)
        do("dve", lambda e: e.tensor_tensor(a_t, psc[:, :, 0, :], a_t, ALU.add), [("a", "part")], ("as", 0))
        do("dve", lambda e: e.tensor_tensor(a_t, a_t, dec_t, ALU.mult), [("as", 0), ("dec", 0)], ("ad", 0))
        do("dve", lambda e: e.scalar_tensor_tensor(xr[:, 7, :], xr[:, 7, :], -1.0, xr[:, 7, :], ALU.mult, ALU.max),
           [("ad", 0)], ("ad", 1))
        do("dve", lambda e: e.tensor_scalar(a_sb[0][:, :], xr[:, 7, :], 1.0, None, ALU.max), [("ad", 1)], ("ahi", 0))
        do("dve", lambda e: e.scalar_tensor_tensor(a_sb[1][:, :], xr[:, 7, :], 1.0, f(a_sb[0][:, :]), ALU.max,
                                                   ALU.subtract), [("ahi", 0)], ("alo", 0))
        w_store(LATE - 1)
        v_out(B - 1)
        v_store(B - 1)
        x_again(1)
        do("dve", lambda e: e.tensor_copy(flag[:, :], ptb[0:1, 0, 0:1]), [("lows", 0)], ("flag", 0))
        wo_lo(2)
        wo_lo(3)
        do("act", lambda e: e.activation(tg[:, :], colsb[:, 2 * NI:2 * NI + 2], ACT.Tanh), [("cols", 0)], ("tg", 0))

        def o(q, p):
            after = [("vlo", p), ("alo", 0)] + ([("y1", 2 * p - 1)] if p else [])

            def make(e, *_):
                for h in range(4):
                    last = three(e, po[:, h // 2, :, 128 * (h % 2):128 * (h % 2) + 128], [p[:, h, :] for p in a_parts],
                                 [p_[:, :, 128 * h:128 * h + 128] for p_ in vs_of(p)], 0, 1)
                return last
            do(q, make, after, ("o", p))

        yb_read = [("vst1", 63)]

        def halves(ap):
            return ap.rearrange("p (a n) -> p a n", a=2)

        def y_stats(t):
            o_t = po[:, :, t % 2, :]
            do("dve", lambda e: e.bn_stats(st[:, t % 4, :], o_t), [("o", t // 2)], ("st", 64 + t))
            do("dve", lambda e: e.bn_aggr(mv[:, t % 8, :], st[:, t % 4, :]), [("st", 64 + t)], ("mv", 64 + t))

        def y_scaled(t):
            o_t = po[:, :, t % 2, :]
            power(("rs", 64 + t), rs[:, t % 8:t % 8 + 1], mv[:, t % 8, 1:2], 1e-3, [("mv", 64 + t)])
            do("dve", lambda e: e.scalar_tensor_tensor(halves(yb), o_t, mv[:, t % 8, 0:1], halves(gamma), ALU.subtract,
                                                       ALU.mult), [("mv", 64 + t), ("rows", 0), yb_read[0]], ("y1", t))
            yb_read[0] = ("wy", t)

        def y_first(t):
            y_stats(t)
            y_scaled(t)

        def y_second(t):
            do("dve", lambda e: e.scalar_tensor_tensor(yb, yb, rs[:, t % 8:t % 8 + 1], beta, ALU.mult, ALU.add),
               [("y1", t), ("rs", 64 + t)], ("y2", t))
            w_t = raw[:, 2 + t % 2, :]
            do("dve", lambda e: e.tensor_tensor(w_t, w_t, yb, ALU.mult), [("y2", t), (f"wl{t % 2}", t)], ("wy", t))

        def wy_t(q, t):
            transpose(q, ("wy", t), raw[:, 2 + t % 2, :], [("wy", t)] + ([("vev", B - 1)] if t == 1 else []))

        def wy_hi(t):
            before = {0: [], 1: [("w", LATE - 1)], 2: [("wo", 0)], 3: [("wo", 1)]}.get(t, [("wo", t - 1)])
            transposed_hi(("wy", t), wyt_of(t)[0][:, :, :], before)

        def wy_lo(t):
            transposed_lo(("wy", t), wyt_of(t)[1][:, :, :], wyt_of(t)[0][:, :, :])

        def wo_mm(q, t):
            before = {0: ("wev", LATE - 1), 1: ("vev", B - 1), 2: ("x1", 0), 3: ("x1", 1)}.get(t, ("x1", t - 1))
            after = [("tbe", ("wy", t)), ("wolo", 3), before]

            def make(e, *_):
                for k in range(4):
                    last = three(e, py(t), [p[:, k, :] for p in wyt_of(t)], [p[k] for p in wos], k, 4)
                return last
            do(q, make, after, ("wo", t))

        def x1(t):
            x_t = xr[:, t % 8, :]
            do("dve", lambda e: e.scalar_tensor_tensor(x_t, py(t), tg[:, 0:1], x_t, ALU.mult, ALU.add),
               [("wo", t), (f"xa{t // 2 % 4}", t // 2), ("tg", 0)], ("x1", t))

        def stats2(t):
            do("dve", lambda e: e.bn_stats(st2[:, t % 4, :], xr[:, t % 8, :]), [("x1", t)], ("st2", t))
            do("dve", lambda e: e.bn_aggr(mv2[:, t % 8, :], st2[:, t % 4, :]), [("st2", t)], ("mv2", t))
            power(("rs2", t), rs2[:, t % 8:t % 8 + 1], mv2[:, t % 8, 1:2], 1e-5, [("mv2", t)])

        def norm2(t):
            after = [("rs2", t), ("mv2", t), ("x1", t)] + ([("tb", ("x2", t - 2))] if t >= 2 else [])
            do("dve", lambda e: e.tensor_scalar(xn[:, t % 2, :], xr[:, t % 8, :], mv2[:, t % 8, 0:1],
                                                rs2[:, t % 8:t % 8 + 1], ALU.subtract, ALU.mult), after, ("xn2", t))

        def x2_dst(t):
            return [p[:, :, 128 * (t % 4):128 * (t % 4) + 128] for p in x2t]

        def x2_t(q, t):
            transpose(q, ("x2", t), xn[:, t % 2, :], [("xn2", t)])

        def slot_free(n):
            g, j = divmod(n, 15)
            return ("h", 11 * g + j) if j < 11 else ("oe", 4 * g + j - 11)

        def product(e, exact, dst, lhs, rhs, k, n, left):
            act, wt = (rhs, lhs) if left else (lhs, rhs)
            if exact:
                pairs = [(wt, act[0]), (wt, act[1])]
            else:
                pairs = [(f(wt), f(act[0])), (wt, act[1])]
            for i, (a, b) in enumerate(pairs):
                p = (a, b) if left else (b, a)
                last = e.matmul(dst, p[0], p[1], start=(k == 0 and i == 0), stop=(k == n - 1 and i == 1))
            return last

        def up_mm(g, j):
            n, m = 15 * g + j, 11 * g + j
            for which, (wt, kind) in enumerate(((gate, "gm"), (up, "um"))):
                after = []
                if which == 0:
                    if j == 0:
                        after += [("tbe", ("x2", 4 * g + 3))]
                        if g == 0:
                            after += [(f"wld{c}", 0) for c in range(8)] + [("wev", 62), ("wev", 63), ("as", 0), ("flag", 0)]
                    if n >= 2:
                        after.append(slot_free(n - 2))

                def make(e, exact, which=which, wt=wt):
                    for k in range(4):
                        last = product(e, exact, banks[2 * (n % 2) + which], wt[:, k, 128 * j:128 * j + 128],
                                       [x2t[0][:, k, :], x2t[1][:, k, :]], k, 4, True)
                    return last
                do("pe2", make, after, (kind, m))

        def silu(g, j):
            m, n = 11 * g + j, 15 * g + j
            after = [("gm", m)]
            after += [("hlo", m - 3)] if m >= 3 else [("wst0", 62), ("wst1", 63)]
            do("act", lambda e: e.activation(tmp[:, m % 3, :], banks[2 * (n % 2)], ACT.Silu,
                                             scale=colsb[:, j:j + 1]), after, ("si", m))

        def hidden(g, j):
            m, n = 11 * g + j, 15 * g + j
            s_t = tmp[:, m % 3, :]
            do("dve", lambda e: e.scalar_tensor_tensor(s_t, banks[2 * (n % 2) + 1], colsb[:, NI + j:NI + j + 1], s_t,
                                                       ALU.mult, ALU.mult), [("si", m), ("um", m)], ("h", m))

        def hidden_hi(g, j):
            m = 11 * g + j
            high(("hhi", m), hid[0][:, j, :], tmp[:, m % 3, :], [("h", m)])

        def hidden_lo(g, j):
            m = 11 * g + j
            rest(("hlo", m), hid[1][:, j, :], tmp[:, m % 3, :], hid[0][:, j, :], [("hhi", m)])

        def down_mm(g, t):
            n = 15 * g + 11 + t
            sl = slice(128 * t, 128 * t + 128)

            def make(e, exact, lo=0, hi=NI):
                for i in range(lo, hi):
                    last = product(e, exact, banks[2 * (n % 2)], [hid[0][:, i, sl], hid[1][:, i, sl]],
                                   down[:, i, :], i, NI, False)
                return last
            after = [slot_free(n - 2), ("hlo", 11 * g + 9)] + ([("dld", 0)] if g == 0 else [])
            do("pe2", lambda e, exact: make(e, exact, 0, NI - 1), after)
            do("pe2", lambda e, exact: make(e, exact, NI - 1, NI), [("hlo", 11 * g + 10)], ("dn", 4 * g + t))

        def finish(t):
            g, j = divmod(t, 4)
            n = 15 * g + 11 + j
            do("dve", lambda e: e.tensor_tensor(yb, banks[2 * (n % 2)], ds, ALU.mult),
               [("dn", t), ("ds", 0), yb_read[0]], ("oe", t))
            yb_read[0] = ("of", t)
            do("dve", lambda e: e.tensor_tensor(xr[:, t % 8, :], xr[:, t % 8, :], yb, ALU.add), [("oe", t), ("xn2", t)],
               ("of", t))

        def out_store(q):
            dma((f"out{q % 4}", q), out_v[:, 2 * q:2 * q + 2, :], xr[:, 2 * q % 8:2 * q % 8 + 2, :], [("of", 2 * q + 1)])

        def att_pe(q, g, s):
            a, p = 4 * g, 2 * g
            for step, make in ((0, lambda: o(q, p)), (2, lambda: wy_t(q, a)), (3, lambda: wo_mm(q, a)),
                               (3, lambda: wy_t(q, a + 1)), (4, lambda: wo_mm(q, a + 1)), (5, lambda: o(q, p + 1)),
                               (7, lambda: wy_t(q, a + 2)), (8, lambda: wo_mm(q, a + 2)), (8, lambda: wy_t(q, a + 3)),
                               (9, lambda: wo_mm(q, a + 3)), (11, lambda: x2_t(q, a)), (12, lambda: x2_t(q, a + 1)),
                               (13, lambda: x2_t(q, a + 2)), (14, lambda: x2_t(q, a + 3))):
                if step == s:
                    make()

        def att_act(g, s):
            a, p = 4 * g, 2 * g
            if s in (2, 3, 7, 8):
                wy_hi(a + {2: 0, 3: 1, 7: 2, 8: 3}[s])
            if s == 4:
                v_hi(p + 1)
            if s == 11 and g + 1 < NG:
                v_hi(p + 2)
            if s >= 11:
                t = a + s - 11
                transposed_hi(("x2", t), x2_dst(t)[0])

        def att_dve(g, s, end):
            a, p = 4 * g, 2 * g
            if not end:
                if s in (2, 3, 7, 8):
                    wy_lo(a + {2: 0, 3: 1, 7: 2, 8: 3}[s])
                if s >= 11:
                    t = a + s - 11
                    transposed_lo(("x2", t), x2_dst(t)[1], x2_dst(t)[0])
                return
            if s in (2, 7):
                y_second(a + {2: 1, 7: 3}[s])
            if s in (0, 1, 5, 6):
                y_first(a + {0: 0, 1: 1, 5: 2, 6: 3}[s])
            if s in (3, 4, 8, 9):
                x1(a + {3: 0, 4: 1, 8: 2, 9: 3}[s])
                stats2(a + {3: 0, 4: 1, 8: 2, 9: 3}[s])
            if s == 4:
                v_lo(p + 1)
            if s == 11 and g + 1 < NG:
                v_lo(p + 2)
            if 9 <= s <= 12:
                norm2(a + s - 9)

        def att_sp(g, s):
            a, p = 4 * g, 2 * g
            if s == 1 and g:
                x_again(2 * g)
            if s == 2:
                v_load(p + 1)
            if s == 3:
                w_load(a + 2)
            if s == 4:
                w_load(a + 3)
                if g:
                    x_again(2 * g + 1)
            if s == 6 and g + 1 < NG:
                v_load(p + 2)
            if s == 8 and g + 1 < NG:
                w_load(a + 4)
            if s == 9 and g + 1 < NG:
                w_load(a + 5)

        def w_late(t):
            w(t)
            w_out(t)
            w_store(t)

        def wy_all(t):
            wy_t("pe", t)
            wy_hi(t)
            wy_lo(t)

        def x2_all(t):
            x2_t("pe", t)
            transposed_hi(("x2", t), x2_dst(t)[0])
            transposed_lo(("x2", t), x2_dst(t)[1], x2_dst(t)[0])

        def x1_all(t):
            x1(t)
            stats2(t)

        v_hi(1)
        v_lo(1)
        v_load(2)
        w_late(LATE)
        o("pe", 0)
        y_stats(0)
        y_stats(1)
        y_scaled(0)
        y_second(0)
        w_late(LATE + 1)
        y_scaled(1)
        w_late(LATE + 2)
        wy_t("pe", 0)
        wy_hi(0)
        w_load(2)
        o("pe", 1)
        y_second(1)
        wy_lo(0)
        wy_t("pe", 1)
        w_load(3)
        wy_hi(1)
        wo_mm("pe", 0)
        y_stats(2)
        y_stats(3)
        y_scaled(2)
        wy_lo(1)
        wo_mm("pe", 1)
        y_second(2)
        wy_t("pe", 2)
        wy_hi(2)
        x1(0)
        y_scaled(3)
        wy_lo(2)
        stats2(0)
        y_second(3)
        wo_mm("pe", 2)
        wy_t("pe", 3)
        wy_hi(3)
        w_load(4)
        w_load(5)
        x1(1)
        wy_lo(3)
        norm2(0)
        stats2(1)
        x2_t("pe", 0)
        transposed_hi(("x2", 0), x2_dst(0)[0])
        v_hi(2)
        wo_mm("pe", 3)
        norm2(1)
        transposed_lo(("x2", 0), x2_dst(0)[1], x2_dst(0)[0])
        x1_all(2)
        x2_t("pe", 1)
        transposed_hi(("x2", 1), x2_dst(1)[0])
        transposed_lo(("x2", 1), x2_dst(1)[1], x2_dst(1)[0])
        norm2(2)
        w_late(LATE + 3)
        v_lo(2)
        x1_all(3)
        x2_t("pe", 2)
        transposed_hi(("x2", 2), x2_dst(2)[0])
        transposed_lo(("x2", 2), x2_dst(2)[1], x2_dst(2)[0])
        o("pe", 2)
        norm2(3)
        x2_all(3)
        dma(("dld", 0), f(down), down_s.rearrange("(i p) n -> p i n", p=128),
            [(f"scr{c}", 0) for c in range(8, 12)] + [("w", B - 1), ("v", B - 1)])
        do("dve", lambda e: e.tensor_scalar(ds, ds, tg[:, 1:2], None, ALU.mult), [("rows", 0), ("tg", 0)], ("ds", 0))

        for g in range(NG):
            nxt = g + 1 < NG
            for s in range(15):
                if nxt and (g or s):
                    att_pe("pe2", g + 1, s)
                if s < 11:
                    up_mm(g, s)
                else:
                    down_mm(g, s - 11)
                if nxt:
                    att_act(g + 1, s)
                if nxt and s in (1, 6):
                    y_second(4 * (g + 1) + (0 if s == 1 else 2))
                if 1 <= s <= 11:
                    hidden(g, s - 1)
                    hidden_hi(g, s - 1)
                if s < 11:
                    silu(g, s)
                if nxt:
                    att_dve(g + 1, s, False)
                if 1 <= s <= 11:
                    hidden_lo(g, s - 1)
                if s == 0 and g:
                    finish(4 * g - 1)
                    out_store(2 * g - 1)
                if s >= 12:
                    finish(4 * g + s - 12)
                if nxt:
                    att_dve(g + 1, s, True)
                    att_sp(g + 1, s)
                if s == 13:
                    out_store(2 * g)
                if s == 14 and not nxt:
                    dma(("outb", 0), out_v[:, 4 * g + 2, :], xr[:, (4 * g + 2) % 8, :], [("of", 4 * g + 2)])
        finish(4 * NG - 1)
        last = 4 * NG - 1
        dma(("out3", 2 * NG - 1), out_v[:, last, :], xr[:, last % 8, :], [("of", last)])
        do("sp", lambda e: None, [(f"out{q % 4}", q) for q in range(2 * NG - 4, 2 * NG)] + [("outb", 0)])

        sems = {kind: stack.enter_context(nc.semaphore(f"s_{kind}")) for kind in plan.total}
        block = stack.enter_context(nc.Block())

        @block.sync
        def _(e):
            plan.emit("sp", e, sems, {})

        @block.scalar
        def _(e):
            plan.emit("act", e, sems, {})

        @block.vector
        def _(e):
            plan.emit("dve", e, sems, {})

        @block.gpsimd
        def _(e):
            plan.emit("pool", e, sems, {})

        @block.tensor
        def _(e):
            seen = {}
            plan.emit("pe", e, sems, seen)
            e.wait_ge(sems["flag"], plan.value[("flag", 0)])
            some_low = e.alloc_register("some_low")
            e.reg_load(some_low, flag[0:1, 0:1])
            with e.If_eq(some_low, 0):
                plan.emit("pe2", e, sems, dict(seen), True)
            with e.Else():
                plan.emit("pe2", e, sems, dict(seen), False)


def decay_t():
    gam = np.float32(1.0) - np.float32(2.0) ** (-5.0 - np.arange(H, dtype=np.float32))
    idx = np.arange(S, dtype=np.float32)
    expo = idx[None, :] - idx[:, None]
    m = np.where(expo[None] <= 0, gam[:, None, None].astype(np.float64) ** np.minimum(expo, 0)[None], 0.0)
    m = m / np.sqrt(m.sum(axis=-1))[:, None, :] / np.sqrt(float(HD))
    return np.ascontiguousarray(m.transpose(2, 0, 1).reshape(S, H * S).astype(np.float32))


def kernel(x, ctx_2048, g_xattn, g_ffn, L0_xattn_Wh, L0_xattn_wg_w, L0_xattn_wo_w, L0_xattn_gn_gamma, L0_xattn_gn_beta,
           L0_ffn_gate_w, L0_ffn_up_w, L0_ffn_down_w, L0_ffn_gate_s, L0_ffn_up_s, L0_ffn_down_s):
    import numpy as _np
    import concourse.bacc as _bacc
    from concourse import mybir as _mybir
    from concourse.bass_utils import run_bass_kernel_spmd as _run

    def laid(a):
        return _np.ascontiguousarray(a)

    c = {k: _np.asarray(v) for k, v in dict(
        x=x, ctx=ctx_2048, gx=g_xattn, gf=g_ffn, wh=L0_xattn_Wh, wg=L0_xattn_wg_w, wo=L0_xattn_wo_w,
        gamma=L0_xattn_gn_gamma, beta=L0_xattn_gn_beta, gw=L0_ffn_gate_w, uw=L0_ffn_up_w, dw=L0_ffn_down_w,
        gs=L0_ffn_gate_s, us=L0_ffn_up_s, ds=L0_ffn_down_s).items()}
    arrays = {
        "in_x": laid(c["x"]),
        "in_ctx_t": laid(c["ctx"].transpose(2, 0, 1).reshape(D, B * S)),
        "in_wh": laid(c["wh"]),
        "in_wh_t": laid(c["wh"].transpose(0, 2, 1)),
        "in_wg": laid(c["wg"]),
        "in_wo": laid(c["wo"]),
        "in_gate_t": laid(c["gw"].T),
        "in_up_t": laid(c["uw"].T),
        "in_down_t": laid(c["dw"].T),
        "in_cols": laid(_np.concatenate([c["gs"].reshape(NI, 128).T, c["us"].reshape(NI, 128).T,
                                         _np.broadcast_to(c["gx"][0:1], (128, 1)),
                                         _np.broadcast_to(c["gf"][0:1], (128, 1))], axis=1)),
        "in_rows": laid(_np.broadcast_to(_np.stack([c["gamma"], c["beta"], c["ds"]]), (128, 3, D))),
        "in_decay": decay_t(),
        "in_eye": _np.eye(128, dtype=_np.float32),
    }
    nc = _bacc.Bacc("TRN2", target_bir_lowering=False, num_devices=1)
    args = [nc.dram_tensor(n, a.shape, _mybir.dt.from_np(a.dtype), kind="ExternalInput").ap() for n, a in arrays.items()]
    args.append(nc.dram_tensor("out", (B, S, D), _mybir.dt.float32, kind="ExternalOutput").ap())
    gated_layer(nc, *args)
    r = _run(nc, [arrays], core_ids=[0])
    return r.results[0]["out"]
```

```python
import numpy as np
import concourse.bass as bass
from concourse import mybir
from contextlib import ExitStack

B, S, D, H, HD, NI = 64, 128, 512, 4, 128, 11
INTER = NI * 128
NG = B // 4
LATE = B - 4


class Plan:

    def __init__(self):
        self.queue, self.total, self.value = {}, {}, {}

    def do(self, engine, make, after=(), then=None, inc=1):
        if then is not None:
            kind = then[0]
            self.total[kind] = self.total.get(kind, 0) + inc
            assert then not in self.value
            self.value[then] = self.total[kind]
        self.queue.setdefault(engine, []).append((tuple(after), make, then, inc))

    def emit(self, name, engine, sems, seen, *args):
        for after, make, then, inc in self.queue.get(name, ()):
            for event in after:
                value = self.value[event]
                if seen.get(event[0], 0) < value:
                    seen[event[0]] = value
                    engine.wait_ge(sems[event[0]], value)
            made = make(engine, *args)
            if then is not None:
                made.then_inc(sems[then[0]], inc)


def gated_layer(nc, x, ctx_t, wh, wh_t, wg, wo, gate_t, up_t, down_t, cols, rows, decay, eye, out):
    f32, f32r, u32, i32 = mybir.dt.float32, mybir.dt.float32r, mybir.dt.uint32, mybir.dt.int32
    ALU = mybir.AluOpType
    ACT = mybir.ActivationFunctionType
    AX = mybir.AxisListType

    stack = ExitStack()
    with stack:
        def sb(name, shape, dt=f32):
            return stack.enter_context(nc.sbuf_tensor(name, shape, dt))

        gate = sb("gate", [128, 4, INTER], f32r)
        up = sb("up", [128, 4, INTER], f32r)
        xreg = sb("xreg", [128, NI * 512], f32r)
        wgs = [xreg[:, 2048 * i:2048 * i + 2048].rearrange("p (k n) -> p k n", k=4) for i in range(2)]
        gs_ = [xreg[:, 4096 + 512 * i:4608 + 512 * i].rearrange("p (h n) -> p h n", h=4) for i in range(2)]
        acc_sb = sb("acc", [128, 512])
        acc = acc_sb[:, :]
        down = xreg[:, 0:NI * 512].rearrange("p (i n) -> p i n", i=NI)
        a_sb = [sb(f"a{i}", [128, 512], f32r) for i in range(2)]
        a_parts = [a[:, :].rearrange("p (h n) -> p h n", h=4) for a in a_sb]
        reg = sb("reg", [128, 84 * 256], f32r)

        def part(kib, n, **dims):
            v = reg[:, 256 * kib:256 * kib + n * int(np.prod(list(dims.values())))]
            names = list(dims)
            return v.rearrange(f"p ({' '.join(names)} n) -> p {' '.join(names)} n", **dims)

        xnt = [[part(16 * b + 8 * i, 512, k=4) for i in range(2)] for b in range(2)]
        whs = part(32, 128, q=2, h=4)
        zt = part(36, 512, q=2, h=4)
        ct = [[part(52 + 16 * b + 8 * i, 512, h=4) for i in range(2)] for b in range(2)]

        def wh_and_z(q, h, b):
            at = 8192 + 512 * q + 128 * h
            apart = 1024 + 1536 * q + 384 * h + 128 * b
            return reg[:, at:at + 2 * apart].rearrange("p (a n) -> p a n", a=2)[:, :, 0:128]

        hid = [part(22 * i, 512, i=NI) for i in range(2)]
        vs = [part(52 + 4 * i, 512, b=2) for i in range(2)]
        x2t = [part(68 + 8 * i, 512, k=4) for i in range(2)]
        wos = [[reg[:, 256 * kib:256 * kib + 512] for kib in (60, 62, 64, 66)],
               [reg[:, 256 * kib:256 * kib + 512] for kib in (44, 46, 48, 50)]]
        wyt = [sb(f"wyt{i}", [128, 4, 128], f32r) for i in range(2)]
        vs_first = [part(4 + 4 * i, 512, b=2) for i in range(2)]
        wyt_first = [part(2 * i, 128, k=4) for i in range(2)]

        xr = sb("xr", [128, 8, 512])
        xn = sb("xn", [128, 2, 512])
        tmp = sb("tmp", [128, 4, 512])
        raw = sb("raw", [128, 4, 512])
        stg = sb("stg", [128, 704])
        colsb = sb("colsb", [128, 2 * NI + 2])
        rowsb = sb("rowsb", [128, 3, 512])
        ident = sb("ident", [128, 128])
        tg = sb("tg", [128, 2])
        st = sb("st", [128, 4, 6])
        mv = sb("mv", [128, 8, 2])
        rs = sb("rs", [128, 8])
        st2 = sb("st2", [128, 4, 6])
        mv2 = sb("mv2", [128, 8, 2])
        rs2 = sb("rs2", [128, 8])
        low = sb("low", [128, 24])
        lowm = sb("lowm", [128, 1])
        ones = sb("ones", [128, 1])
        nhalf = sb("nhalf", [128, 1])
        flag = sb("flag", [1, 1], i32)
        gamma, beta, ds = rowsb[:, 0, :], rowsb[:, 1, :], rowsb[:, 2, :]
        yb = tmp[:, 3, :]

        ps = [stack.enter_context(nc.psum_tensor(f"ps{i}", [128, 4, 2, 128], f32)) for i in range(2)]
        banks = [p[:, 2 * i:2 * i + 2, :, :].rearrange("p a b n -> p (a b n)") for p in ps for i in range(2)]
        po = stack.enter_context(nc.psum_tensor("po", [128, 2, 2, 256], f32))
        ptb = stack.enter_context(nc.psum_tensor("ptb", [128, 4, 128], f32))
        pyb = stack.enter_context(nc.psum_tensor("pyb", [128, 512], f32))
        pz = [po[:, i, :, :].rearrange("p a n -> p (a n)") for i in range(2)]

        v_s = nc.dram_tensor("v_scratch", [128, B, D], f32, kind="Internal").ap()
        w_s = nc.dram_tensor("w_scratch", [128, B, D], f32, kind="Internal").ap()
        gate_s = nc.dram_tensor("gate_scratch", [D, INTER], f32, kind="Internal").ap()
        up_s = nc.dram_tensor("up_scratch", [D, INTER], f32, kind="Internal").ap()
        down_s = nc.dram_tensor("down_scratch", [INTER, D], f32, kind="Internal").ap()

        x_v = x.rearrange("b s d -> s b d")
        out_v = out.rearrange("b s d -> s b d")
        ct_v = ctx_t.rearrange("(h p) n -> p h n", p=128)
        down_flat = down_t.rearrange("(p a) n -> p (a n)", p=128)

        plan = Plan()
        do = plan.do

        def f(ap):
            return ap.bitcast(f32)

        def dma(key, dst, src, after=()):
            do("sp", lambda e: e.dma_start(dst, src), after, key, 16)

        def high(key, dst, src, after):
            do("act", lambda e: e.copy(dst, src), after, key)

        def rest(key, dst, src, hi, after):
            do("dve", lambda e: e.tensor_tensor(dst, src, f(hi), ALU.subtract), after, key)

        def three(e, dst, lhs, rhs, k, n):
            for i, (a, b) in enumerate(((0, 0), (0, 1), (1, 0))):
                last = e.matmul(dst, lhs[a], rhs[b], start=(k == 0 and i == 0), stop=(k == n - 1 and i == 2))
            return last

        def x_load(q):
            after = [("xn", 2 * q - 7)] if q >= 4 else []
            if q == 3:
                after = [("whlo", 0), ("G", 0)]
            dma((f"xl{q % 4}", q), xr[:, 2 * q % 8:2 * q % 8 + 2, :], x_v[:, 2 * q:2 * q + 2, :], after)

        def stats(t):
            do("dve", lambda e: e.bn_stats(st[:, t % 4, :], xr[:, t % 8, :]),
               [(f"xl{t // 2 % 4}", t // 2) if t else ("xf", 0)], ("st", t))
            do("dve", lambda e: e.bn_aggr(mv[:, t % 8, :], st[:, t % 4, :]), [("st", t)], ("mv", t))

        def power(key, dst, var, eps, after):
            do("pool", lambda e: e.tensor_scalar(dst, var, eps, None, ALU.add), after, ("eps", key))
            do("pool", lambda e: e.tensor_tensor(dst, dst, nhalf[:, :], ALU.pow), [("eps", key), ("ones", 1)], key)

        def rstd(t):
            power(("rs", t), rs[:, t % 8:t % 8 + 1], mv[:, t % 8, 1:2], 1e-5, [("mv", t)])

        def norm(t):
            after = [("rs", t), ("mv", t)] + ([("tb", ("x", t - 2))] if t >= 2 else [])
            do("dve", lambda e: e.tensor_scalar(xn[:, t % 2, :], xr[:, t % 8, :], mv[:, t % 8, 0:1],
                                                rs[:, t % 8:t % 8 + 1], ALU.subtract, ALU.mult), after, ("xn", t))

        tb_last = {}

        tb_banks = [ptb[:, :, :], pyb[:, :].rearrange("p (k n) -> p k n", k=4)]
        tb_banks += [p[:, 2 * i:2 * i + 2, :, :].rearrange("p a b n -> p (a b) n")
                     for p in (ps[1], ps[0]) for i in range(2)]
        tb_elsewhere = {("x", 1): 2, ("x", 2): 3, ("x", 3): 1, ("wy", 1): 5, ("wy", 3): 5, ("x2", 1): 5, ("x2", 3): 5}

        def tb_of(key):
            return tb_banks[tb_elsewhere.get(key, 0)]

        def transpose(q, key, src, after):
            bank, place = tb_of(key), tb_elsewhere.get(key, 0)
            if tb_last.get(place):
                after = [*after, ("tbe", tb_last[place])]
            tb_last[place] = key

            def make(e, *_):
                for k in range(4):
                    last = e.transpose(bank[:, k, :], src[:, 128 * k:128 * k + 128], ident[:, :])
                return last
            do(q, make, after, ("tb", key))

        def transposed_hi(key, dst, after=()):
            high(("tbh", key), dst, tb_of(key), [("tb", key), *after])

        def transposed_lo(key, dst, hi):
            rest(("tbe", key), dst, tb_of(key), hi, [("tbh", key)])

        def xt_dst(t):
            return [p[:, :, 128 * (t % 4):128 * (t % 4) + 128] for p in xnt[t // 4 % 2]]

        def xt(t):
            transpose("pe", ("x", t), xn[:, t % 2, :], [("xn", t), ("c", "eye")])

        def xt_hi(t):
            transposed_hi(("x", t), xt_dst(t)[0])

        def xt_lo(t):
            transposed_lo(("x", t), xt_dst(t)[1], xt_dst(t)[0])

        def z(g, h):
            after = [("tbe", ("x", 4 * g + 3)), ("Glo", 0)]
            n = 4 * g + h
            if n >= 2:
                after.append(("zlo", n - 2))
            operands = [[p[:, h, :] for p in parts] for parts in (gs_, xnt[g % 2])]
            do("pe", lambda e, *_: three(e, pz[h % 2], *operands, 0, 1), after, ("z", n))

        def z_hi(g, h):
            high(("zhi", 4 * g + h), zt[:, 0, h, :], pz[h % 2], [("z", 4 * g + h)])

        def z_lo(g, h):
            rest(("zlo", 4 * g + h), zt[:, 1, h, :], pz[h % 2], zt[:, 0, h, :], [("zhi", 4 * g + h)])

        def ct_load(g, hp):
            after = [("ctlo", (g - 1, 2 * hp + 1))] if g else []
            dma((f"ct{hp}", g), raw[:, 2 * hp:2 * hp + 2, :], ct_v[:, 2 * hp:2 * hp + 2, 512 * g:512 * g + 512], after)

        def ct_split(g, h, first=False):
            a, b = ct[g % 2][0][:, h, :], ct[g % 2][1][:, h, :]
            after = [(f"ct{h // 2}", g)] + ([("v", 4 * g - 5)] if g >= 2 else [])
            do("act" if first else "pool", lambda e: (e.copy if first else e.tensor_copy)(a, raw[:, h, :]),
               after, ("cthf" if first else "cthi", (g, h)))
            do("dve" if first else "pool", lambda e: e.tensor_tensor(b, raw[:, h, :], f(a), ALU.subtract),
               [("cthf" if first else "cthi", (g, h))], ("ctlo", (g, h)) if not first else ("ctlf", (g, h)))

        def ct_ready(g):
            return [("ctlo", (g, 3))] + ([("ctlf", (0, 1))] if g == 0 else [])

        def v(t, half):
            g, b = divmod(t, 4)
            after = [("zlo", 4 * g + 2 * half + 1), *ct_ready(g), ("whlo", 0)]
            if t >= 2:
                after += [("vev", t - 2), ("acc", t - 2)]

            def make(e, *_):
                for h in (2 * half, 2 * half + 1):
                    for n, (i, q) in enumerate(((0, 0), (1, 0), (0, 1))):
                        last = e.matmul(ps[t % 2][:, h, :, :], ct[g % 2][i][:, h, 128 * b:128 * b + 128],
                                        wh_and_z(q, h, b), start=(n == 0), stop=(n == 2))
                return last
            do("pe", make, after, ("v", t) if half else None)

        def v_out(t):
            dst = tmp[:, 2 + t % 2, :].rearrange("p (h n) -> p h n", h=4)
            after = [("v", t)] + ([(f"vst{t % 2}", t - 2)] if t >= 2 else [("wglo", 2 + t)])
            do("act", lambda e: e.copy(dst, ps[t % 2][:, :, 0, :]), after, ("vev", t))
            acc_t = acc.rearrange("p (h n) -> p h n", h=4)
            if t:
                do("dve", lambda e: e.tensor_tensor(acc_t, acc_t, ps[t % 2][:, :, 1, :], ALU.add),
                   [("vev", t), ("acc", t - 1)], ("acc", t))
            else:
                do("dve", lambda e: e.tensor_copy(acc_t, ps[0][:, :, 1, :]), [("vev", 0)], ("acc", 0))

        def v_store(t):
            dma((f"vst{t % 2}", t), v_s[:, t, :], tmp[:, 2 + t % 2, :], [("vev", t)])

        def pw(t):
            return pyb[:, :] if t < LATE else banks[2 + t % 2]

        def w(t):
            after = [("tbe", ("x", t)), ("wglo", 3 if t else 0)] + ([("wev", t - (2 if t >= LATE else 1))] if t else [])
            if t >= LATE:
                after += [("acc", B - 1), ("vev", B - 1)]

            def make(e, ks):
                sl = slice(128 * (t % 4), 128 * (t % 4) + 128)
                for k in ks:
                    last = three(e, pw(t), [p[:, k, sl] for p in xnt[t // 4 % 2]], [p[:, k, :] for p in wgs], k, 4)
                return last
            if t:
                do("pe", lambda e, *_: make(e, range(4)), after, ("w", t))
                return
            for k in range(4):
                do("pe", lambda e, *_, k=k: make(e, (k,)), [("wglo", k)] if k else after,
                   ("w", t) if k == 3 else None)

        def w_out(t):
            after = [("w", t)] + ([(f"wst{t % 2}", t - 2)] if t >= 2 else [("wglo", t)])
            do("act", lambda e: e.activation(tmp[:, t % 2, :], pw(t), ACT.Relu), after, ("wev", t))

        def w_store(t):
            dma((f"wst{t % 2}", t), w_s[:, t, :], tmp[:, t % 2, :], [("wev", t)])

        chunks = ([(gate_t[128 * k:128 * k + 128, :], gate_s[128 * k:128 * k + 128, :], gate[:, k, :]) for k in range(4)]
                  + [(up_t[128 * k:128 * k + 128, :], up_s[128 * k:128 * k + 128, :], up[:, k, :]) for k in range(4)]
                  + [(down_t[352 * k:352 * k + 352, :], down_s[352 * k:352 * k + 352, :], None) for k in range(4)])

        def to_scratch(c):
            src, dst, _ = chunks[c]
            dma((f"scr{c}", 0), dst, src)

        def weight_load(c):
            _, src, dst = chunks[c]
            dma((f"wld{c}", 0), f(dst), src, [(f"scr{c}", 0)])

        def low_load(c, half):
            at = 1408 * (c - 8) + 704 * half
            after = [("low", 2 * c + half - 1)]
            dma(("lowld", 2 * c + half), stg[:, :], down_flat[:, at:at + 704], after)

        def low_bits(c, half):
            n = 2 * c + half
            if c < 8:
                src, after = chunks[c][2][:, 704 * half:704 * half + 704].bitcast(u32), [(f"wld{c}", 0)]
            else:
                src, after = stg[:, :].bitcast(u32), [("lowld", n)]
            do("dve", lambda e: e.tensor_scalar(stg[:, :].bitcast(u32), src, 0xFFF, None, ALU.bitwise_and), after,
               ("and", n))
            do("dve", lambda e: e.tensor_reduce(low[:, n:n + 1], stg[:, :].bitcast(i32), AX.X, ALU.max),
               [("and", n)], ("low", n))

        dma(("xf", 0), xr[:, 0, :], x_v[:, 0, :])
        dma(("c", "eye"), ident[:, :], eye)
        dma(("xl0", 0), xr[:, 1, :], x_v[:, 1, :])
        dma(("whr", 0), xr[:, 6, :].rearrange("p (h n) -> p h n", h=4), wh_t.rearrange("h e d -> e h d"))
        x_load(1)
        ct_load(0, 1)
        dma(("whr2", 0), xr[:, 7, :].rearrange("p (h n) -> p h n", h=4), wh.rearrange("h d e -> d h e"))
        ct_load(0, 0)
        x_load(2)
        dma(("wgr", 0), tmp[:, :, :], wg.rearrange("(k p) n -> p k n", p=128))
        x_load(3)
        dma(("cols", 0), colsb[:, :], cols)
        dma(("rows", 0), rowsb[:, :, :], rows)

        do("pool", lambda e: e.memset(ones[:, :], 1.0), (), ("ones", 0))
        do("pool", lambda e: e.memset(nhalf[:, :], -0.5), (), ("ones", 1))

        def g_make(e, *_):
            wt = xr[:, 6, :].rearrange("p (h n) -> p h n", h=4)
            for h in range(4):
                last = e.matmul(pz[0][:, 128 * h:128 * h + 128], wt[:, h, :], wt[:, h, :], start=True, stop=True)
            return last
        g4 = [xreg[:, 4096 + 512 * i:4608 + 512 * i] for i in range(2)]
        wh_raw = xr[:, 7, :].rearrange("p (h n) -> p h n", h=4)
        stats(0)
        rstd(0)
        stats(1)
        rstd(1)
        norm(0)
        xt(0)
        xt_hi(0)
        stats(2)
        rstd(2)
        do("pe", g_make, [("whr", 0)], ("G", 0))
        norm(1)
        xt(1)
        xt_hi(1)
        stats(3)
        rstd(3)
        high(("Ghi", 0), g4[0], pz[0], [("G", 0)])
        xt_lo(0)
        norm(2)
        xt(2)
        xt_hi(2)
        xt_lo(1)
        norm(3)
        xt(3)
        xt_hi(3)
        rest(("Glo", 0), g4[1], pz[0], g4[0], [("Ghi", 0)])
        xt_lo(2)
        xt_lo(3)
        high(("whhi", 0), whs[:, 0, :, :], wh_raw, [("whr2", 0)])
        rest(("whlo", 0), whs[:, 1, :, :], wh_raw, whs[:, 0, :, :], [("whhi", 0)])
        for h in range(2):
            ct_split(0, h, first=True)
            ct_split(0, h + 2)

        def wg_split(k):
            high(("wghi", k), wgs[0][:, k, :], tmp[:, k, :], [("wgr", 0)])
            rest(("wglo", k), wgs[1][:, k, :], tmp[:, k, :], wgs[0][:, k, :], [("wghi", k)])
        stats(4)
        rstd(4)

        all_read = ("v", B - 1)

        def v_load(p):
            after = [("vlo", p - 1)] if p else [("ctlo", (NG - 1, 3))]
            after += [("vst0", 2 * p), ("vst1", 2 * p + 1)]
            dma(("vld", p), raw[:, 0:2, :], v_s[:, 2 * p:2 * p + 2, :], after)

        def w_load(t):
            after = [("tb", ("wy", t - 2))] if t >= 2 else [("ctlo", (NG - 1, 3))]
            after.append((f"wst{t % 2}", t))
            dma((f"wl{t % 2}", t), raw[:, 2 + t % 2, :], w_s[:, t, :], after)

        def x_again(q):
            if q >= 4:
                after = [(f"out{q % 4}", q - 4)]
            elif q < 2:
                after = [("xn", 2 * q + 57)] + [("ad", 0)] * q
            else:
                after = [("wolo", 3), ("alo", 0)]
            dma((f"xa{q % 4}", q), xr[:, 2 * q % 8:2 * q % 8 + 2, :], x_v[:, 2 * q:2 * q + 2, :], after)

        def vs_of(p):
            return vs_first if p == 1 else vs

        def wyt_of(t):
            return wyt_first if t in (1, 3) else wyt

        def py(t):
            return banks[0] if t in (1, 3) else pyb[:, :]

        def v_hi(p):
            before = {0: ("v", B - 5), 1: ("w", LATE - 1), 2: ("o", 0)}.get(p, ("o", p - 1))
            high(("vhi", p), vs_of(p)[0], raw[:, 0:2, :], [("vld", p), before])

        def v_lo(p):
            rest(("vlo", p), vs_of(p)[1], raw[:, 0:2, :], vs_of(p)[0], [("vhi", p)])

        def wo_hi(k):
            src = xr[:, 4 + k, :] if k < 3 else stg[:, 0:512]
            high(("wohi", k), wos[0][k], src, [("wor", 0) if k < 3 else ("wor3", 0), ("v", B - 5)])

        def wo_lo(k):
            src = xr[:, 4 + k, :] if k < 3 else stg[:, 0:512]
            rest(("wolo", k), wos[1][k], src, wos[0][k], [("wohi", k), all_read])

        for g in range(NG):
            n = 4 * g + 4
            more = g + 1 < NG
            if g == 0:
                for hp in range(2):
                    dma((f"ct{hp}", 1), raw[:, 2 * hp:2 * hp + 2, :], ct_v[:, 2 * hp:2 * hp + 2, 512:1024],
                        [("ctlf", (0, 1)) if hp == 0 else ("ctlo", (0, 3))])
            if g < 12:
                to_scratch(g)
            if 1 <= g <= 8:
                weight_load(g - 1)

            def z_pair(g, h):
                z(g, h)
                z(g, h + 1)
                for i in (h, h + 1):
                    z_hi(g, i)
                    z_lo(g, i)

            def w_all(t):
                w(t)
                w_out(t)
                w_store(t)

            def x_all(j):
                xt(n + j)
                xt_hi(n + j)
                xt_lo(n + j)

            def dve_next(t):
                if t < B:
                    stats(t)
                    rstd(t)

            z_pair(g, 0)
            if g:
                if more:
                    ct_split(g + 1, 0)
                    norm(n + 1)
                w_all(4 * g - (1 if more else 2))
                z_pair(g, 2)
            else:
                norm(4)
                wg_split(0)
                wg_split(1)
                z_pair(0, 2)
                wg_split(2)
                wg_split(3)
                stats(5)
                rstd(5)
                ct_split(1, 0)
                w_all(0)
                norm(5)
            if more:
                x_all(0)
                dve_next(n + 2)
            v(4 * g, 0)
            v(4 * g + 1, 0)
            v(4 * g, 1)
            v_out(4 * g)
            if not more:
                v_load(0)
                v_store(4 * g)
                v(4 * g + 1, 1)
                v_out(4 * g + 1)
                v_store(4 * g + 1)
                dma(("wor", 0), xr[:, 4:7, :], wo.rearrange("(k p) n -> p k n", p=128)[:, 0:3, :], [("xn", 62)])
                v(4 * g + 2, 0)
                v(4 * g + 2, 1)
                v_out(4 * g + 2)
                v_store(4 * g + 2)
                w_load(0)
                v(4 * g + 3, 0)
                v(4 * g + 3, 1)
                v_hi(0)
                v_lo(0)
                v_out(4 * g + 3)
                v_load(1)
                v_store(4 * g + 3)
                w_load(1)
                x_again(0)
                for k in range(4):
                    wo_hi(k)
                w(LATE - 1)
                break
            v(4 * g + 1, 1)
            v_out(4 * g + 1)
            v_store(4 * g)
            if 0 < g < NG - 1:
                ct_load(g + 1, 1)
            x_all(1)
            norm(n + 2)
            dve_next(n + 3)
            if g + 2 < NG:
                x_load(2 * g + 4)
            v_store(4 * g + 1)
            if g < NG - 2:
                w_all(4 * g + (0 if g else 1))
            ct_split(g + 1, 1)
            v(4 * g + 2, 0)
            v(4 * g + 2, 1)
            v_out(4 * g + 2)
            x_all(2)
            norm(n + 3)
            if 2 <= g < 14:
                low_bits(g - 2, 0)
                if g >= 10:
                    low_load(g - 2, 1)
            dve_next(n + 4)
            v_store(4 * g + 2)
            if g:
                w_all(4 * g + (1 if g < NG - 2 else 0))
            ct_split(g + 1, 2)
            v(4 * g + 3, 0)
            v(4 * g + 3, 1)
            v_out(4 * g + 3)
            x_all(3)
            if n + 4 < B:
                norm(n + 4)
            dve_next(n + 5)
            v_store(4 * g + 3)
            if g + 2 < NG:
                ct_load(g + 2, 0)
                x_load(2 * g + 5)
            w_all(4 * g + (2 if g < NG - 2 else 1))
            ct_split(g + 1, 3)
            if 2 <= g < 14:
                low_bits(g - 2, 1)
                if 9 <= g < 13:
                    low_load(g - 1, 0)
            if g == NG - 2:
                do("dve", lambda e: e.tensor_reduce(lowm[:, :], low[:, :], AX.X, ALU.max), [("low", 23)], ("lowm", 0))
                dma(("dec", 0), xr[:, 3, :], decay, [("xn", 59)])
                dma(("wor3", 0), stg[:, 0:512], wo.rearrange("(k p) n -> p k n", p=128)[:, 3, :], [("low", 23)])

        do("pe", lambda e, *_: e.matmul(ptb[0:1, 0, 0:1], lowm[:, :], ones[:, :], start=True, stop=True),
           [("lowm", 0), ("ones", 0), ("tbe", ("x", 63))], ("lows", 0))
        a_t = xr[:, 7, :].rearrange("p (h n) -> p h n", h=4)
        dec_t = xr[:, 3, :].rearrange("p (h n) -> p h n", h=4)
        w_out(LATE - 1)
        do("dve", lambda e: e.tensor_tensor(a_t, acc.rearrange("p (h n) -> p h n", h=4), dec_t, ALU.mult),
           [("acc", B - 1), ("dec", 0), ("xn", B - 1)], ("ad", 0))
        do("dve", lambda e: e.scalar_tensor_tensor(xr[:, 7, :], xr[:, 7, :], -1.0, xr[:, 7, :], ALU.mult, ALU.max),
           [("ad", 0)], ("ad", 1))
        do("dve", lambda e: e.tensor_scalar(a_sb[0][:, :], xr[:, 7, :], 1.0, None, ALU.max), [("ad", 1)], ("ahi", 0))
        do("dve", lambda e: e.scalar_tensor_tensor(a_sb[1][:, :], xr[:, 7, :], 1.0, f(a_sb[0][:, :]), ALU.max,
                                                   ALU.subtract), [("ahi", 0)], ("alo", 0))
        w_store(LATE - 1)
        x_again(1)
        do("dve", lambda e: e.tensor_copy(flag[:, :], ptb[0:1, 0, 0:1]), [("lows", 0)], ("flag", 0))
        wo_lo(0)
        wo_lo(1)
        do("act", lambda e: e.activation(tg[:, :], colsb[:, 2 * NI:2 * NI + 2], ACT.Tanh), [("cols", 0)], ("tg", 0))

        def o(q, p):
            after = [("vlo", p), ("alo", 0)] + ([("y1", 2 * p - 1)] if p else [])

            def make(e, *_):
                for h in range(4):
                    last = three(e, po[:, h // 2, :, 128 * (h % 2):128 * (h % 2) + 128], [p[:, h, :] for p in a_parts],
                                 [p_[:, :, 128 * h:128 * h + 128] for p_ in vs_of(p)], 0, 1)
                return last
            do(q, make, after, ("o", p))

        yb_read = [("vst1", 63)]

        def halves(ap):
            return ap.rearrange("p (a n) -> p a n", a=2)

        def y_stats(t):
            o_t = po[:, :, t % 2, :]
            do("dve", lambda e: e.bn_stats(st[:, t % 4, :], o_t), [("o", t // 2)], ("st", 64 + t))
            do("dve", lambda e: e.bn_aggr(mv[:, t % 8, :], st[:, t % 4, :]), [("st", 64 + t)], ("mv", 64 + t))

        def y_scaled(t):
            o_t = po[:, :, t % 2, :]
            power(("rs", 64 + t), rs[:, t % 8:t % 8 + 1], mv[:, t % 8, 1:2], 1e-3, [("mv", 64 + t)])
            do("dve", lambda e: e.scalar_tensor_tensor(halves(yb), o_t, mv[:, t % 8, 0:1], halves(gamma), ALU.subtract,
                                                       ALU.mult), [("mv", 64 + t), ("rows", 0), yb_read[0]], ("y1", t))
            yb_read[0] = ("wy", t)

        def y_first(t):
            y_stats(t)
            y_scaled(t)

        def y_second(t):
            do("dve", lambda e: e.scalar_tensor_tensor(yb, yb, rs[:, t % 8:t % 8 + 1], beta, ALU.mult, ALU.add),
               [("y1", t), ("rs", 64 + t)], ("y2", t))
            w_t = raw[:, 2 + t % 2, :]
            do("dve", lambda e: e.tensor_tensor(w_t, w_t, yb, ALU.mult), [("y2", t), (f"wl{t % 2}", t)], ("wy", t))

        def wy_t(q, t):
            after = [("wy", t)] + ([("vev", B - 1), ("acc", B - 1)] if t == 1 else [])
            transpose(q, ("wy", t), raw[:, 2 + t % 2, :], after)

        def wy_hi(t):
            before = {0: [], 1: [("w", LATE - 1)], 2: [("wo", 0)], 3: [("wo", 1)]}.get(t, [("wo", t - 1)])
            transposed_hi(("wy", t), wyt_of(t)[0][:, :, :], before)

        def wy_lo(t):
            transposed_lo(("wy", t), wyt_of(t)[1][:, :, :], wyt_of(t)[0][:, :, :])

        def wo_mm(q, t, between=None):
            before = {0: ("wev", LATE - 1), 1: ("vev", B - 1), 2: ("x1", 0), 3: ("x1", 1)}.get(t, ("x1", t - 1))
            after = [("tbe", ("wy", t)), ("wolo", 3), before]

            def make(e, ks):
                for k in ks:
                    last = three(e, py(t), [p[:, k, :] for p in wyt_of(t)], [p[k] for p in wos], k, 4)
                return last
            if between is None:
                do(q, lambda e, *_: make(e, range(4)), after, ("wo", t))
            else:
                do(q, lambda e, *_: make(e, (0, 1)), after)
                between()
                do(q, lambda e, *_: make(e, (2, 3)), (), ("wo", t))

        def x1(t):
            x_t = xr[:, t % 8, :]
            do("dve", lambda e: e.scalar_tensor_tensor(x_t, py(t), tg[:, 0:1], x_t, ALU.mult, ALU.add),
               [("wo", t), (f"xa{t // 2 % 4}", t // 2), ("tg", 0)], ("x1", t))

        def stats2(t):
            do("dve", lambda e: e.bn_stats(st2[:, t % 4, :], xr[:, t % 8, :]), [("x1", t)], ("st2", t))
            do("dve", lambda e: e.bn_aggr(mv2[:, t % 8, :], st2[:, t % 4, :]), [("st2", t)], ("mv2", t))
            power(("rs2", t), rs2[:, t % 8:t % 8 + 1], mv2[:, t % 8, 1:2], 1e-5, [("mv2", t)])

        def norm2(t):
            after = [("rs2", t), ("mv2", t), ("x1", t)] + ([("tb", ("x2", t - 2))] if t >= 2 else [])
            do("dve", lambda e: e.tensor_scalar(xn[:, t % 2, :], xr[:, t % 8, :], mv2[:, t % 8, 0:1],
                                                rs2[:, t % 8:t % 8 + 1], ALU.subtract, ALU.mult), after, ("xn2", t))

        def x2_dst(t):
            return [p[:, :, 128 * (t % 4):128 * (t % 4) + 128] for p in x2t]

        def x2_t(q, t):
            transpose(q, ("x2", t), xn[:, t % 2, :], [("xn2", t)])

        def slot_free(n):
            g, j = divmod(n, 15)
            return ("h", 11 * g + j) if j < 11 else ("oe", 4 * g + j - 11)

        def product(e, exact, dst, lhs, rhs, k, n, left):
            act, wt = (rhs, lhs) if left else (lhs, rhs)
            if exact:
                pairs = [(wt, act[0]), (wt, act[1])]
            else:
                pairs = [(f(wt), f(act[0])), (wt, act[1])]
            for i, (a, b) in enumerate(pairs):
                p = (a, b) if left else (b, a)
                last = e.matmul(dst, p[0], p[1], start=(k == 0 and i == 0), stop=(k == n - 1 and i == 1))
            return last

        def up_mm(g, j):
            n, m = 15 * g + j, 11 * g + j
            for which, (wt, kind) in enumerate(((gate, "gm"), (up, "um"))):
                after = []
                if which == 0:
                    if j == 0:
                        after += [("tbe", ("x2", 4 * g + 3))]
                        if g == 0:
                            after += [(f"wld{c}", 0) for c in range(8)]
                            after += [("wev", 62), ("wev", 63), ("acc", B - 1), ("flag", 0)]
                    if n >= 2:
                        after.append(slot_free(n - 2))

                def make(e, exact, which=which, wt=wt):
                    for k in range(4):
                        last = product(e, exact, banks[2 * (n % 2) + which], wt[:, k, 128 * j:128 * j + 128],
                                       [x2t[0][:, k, :], x2t[1][:, k, :]], k, 4, True)
                    return last
                do("pe2", make, after, (kind, m))

        def silu(g, j):
            m, n = 11 * g + j, 15 * g + j
            after = [("gm", m)]
            after += [("hlo", m - 3)] if m >= 3 else [("wst0", 62), ("wst1", 63)]
            do("act", lambda e: e.activation(tmp[:, m % 3, :], banks[2 * (n % 2)], ACT.Silu,
                                             scale=colsb[:, j:j + 1]), after, ("si", m))

        def hidden(g, j):
            m, n = 11 * g + j, 15 * g + j
            s_t = tmp[:, m % 3, :]
            do("dve", lambda e: e.scalar_tensor_tensor(s_t, banks[2 * (n % 2) + 1], colsb[:, NI + j:NI + j + 1], s_t,
                                                       ALU.mult, ALU.mult), [("si", m), ("um", m)], ("h", m))

        def hidden_hi(g, j):
            m = 11 * g + j
            high(("hhi", m), hid[0][:, j, :], tmp[:, m % 3, :], [("h", m)])

        def hidden_lo(g, j):
            m = 11 * g + j
            rest(("hlo", m), hid[1][:, j, :], tmp[:, m % 3, :], hid[0][:, j, :], [("hhi", m)])

        def down_mm(g, t):
            n = 15 * g + 11 + t
            sl = slice(128 * t, 128 * t + 128)

            def make(e, exact, lo=0, hi=NI):
                for i in range(lo, hi):
                    last = product(e, exact, banks[2 * (n % 2)], [hid[0][:, i, sl], hid[1][:, i, sl]],
                                   down[:, i, :], i, NI, False)
                return last
            after = [slot_free(n - 2), ("hlo", 11 * g + 9)] + ([("dld", 0)] if g == 0 else [])
            do("pe2", lambda e, exact: make(e, exact, 0, NI - 1), after)
            do("pe2", lambda e, exact: make(e, exact, NI - 1, NI), [("hlo", 11 * g + 10)], ("dn", 4 * g + t))

        def finish(t):
            g, j = divmod(t, 4)
            n = 15 * g + 11 + j
            do("dve", lambda e: e.tensor_tensor(yb, banks[2 * (n % 2)], ds, ALU.mult),
               [("dn", t), ("ds", 0), yb_read[0]], ("oe", t))
            yb_read[0] = ("of", t)
            do("dve", lambda e: e.tensor_tensor(xr[:, t % 8, :], xr[:, t % 8, :], yb, ALU.add), [("oe", t), ("xn2", t)],
               ("of", t))

        def out_store(q):
            dma((f"out{q % 4}", q), out_v[:, 2 * q:2 * q + 2, :], xr[:, 2 * q % 8:2 * q % 8 + 2, :], [("of", 2 * q + 1)])

        def att_pe(q, g, s):
            a, p = 4 * g, 2 * g
            for step, make in ((0, lambda: o(q, p)), (2, lambda: wy_t(q, a)), (3, lambda: wo_mm(q, a)),
                               (3, lambda: wy_t(q, a + 1)), (4, lambda: wo_mm(q, a + 1)), (5, lambda: o(q, p + 1)),
                               (7, lambda: wy_t(q, a + 2)), (8, lambda: wo_mm(q, a + 2)), (8, lambda: wy_t(q, a + 3)),
                               (9, lambda: wo_mm(q, a + 3)), (11, lambda: x2_t(q, a)), (12, lambda: x2_t(q, a + 1)),
                               (13, lambda: x2_t(q, a + 2)), (14, lambda: x2_t(q, a + 3))):
                if step == s:
                    make()

        def att_act(g, s):
            a, p = 4 * g, 2 * g
            if s in (2, 3, 7, 8):
                wy_hi(a + {2: 0, 3: 1, 7: 2, 8: 3}[s])
            if s == 4:
                v_hi(p + 1)
            if s == 11 and g + 1 < NG:
                v_hi(p + 2)
            if s >= 11:
                t = a + s - 11
                transposed_hi(("x2", t), x2_dst(t)[0])

        def att_dve(g, s, end):
            a, p = 4 * g, 2 * g
            if not end:
                if s in (2, 3, 7, 8):
                    wy_lo(a + {2: 0, 3: 1, 7: 2, 8: 3}[s])
                if s >= 11:
                    t = a + s - 11
                    transposed_lo(("x2", t), x2_dst(t)[1], x2_dst(t)[0])
                return
            if s in (2, 7):
                y_second(a + {2: 1, 7: 3}[s])
            if s in (0, 1, 5, 6):
                y_first(a + {0: 0, 1: 1, 5: 2, 6: 3}[s])
            if s in (3, 4, 8, 9):
                x1(a + {3: 0, 4: 1, 8: 2, 9: 3}[s])
                stats2(a + {3: 0, 4: 1, 8: 2, 9: 3}[s])
            if s == 4:
                v_lo(p + 1)
            if s == 11 and g + 1 < NG:
                v_lo(p + 2)
            if 9 <= s <= 12:
                norm2(a + s - 9)

        def att_sp(g, s):
            a, p = 4 * g, 2 * g
            if s == 1 and g:
                x_again(2 * g)
            if s == 2:
                v_load(p + 1)
            if s == 3:
                w_load(a + 2)
            if s == 4:
                w_load(a + 3)
                if g:
                    x_again(2 * g + 1)
            if s == 6 and g + 1 < NG:
                v_load(p + 2)
            if s == 8 and g + 1 < NG:
                w_load(a + 4)
            if s == 9 and g + 1 < NG:
                w_load(a + 5)

        def w_late(t):
            w(t)
            w_out(t)
            w_store(t)

        def wy_all(t):
            wy_t("pe", t)
            wy_hi(t)
            wy_lo(t)

        def x2_all(t):
            x2_t("pe", t)
            transposed_hi(("x2", t), x2_dst(t)[0])
            transposed_lo(("x2", t), x2_dst(t)[1], x2_dst(t)[0])

        def x1_all(t):
            x1(t)
            stats2(t)

        v_hi(1)
        v_lo(1)
        v_load(2)
        w_late(LATE)
        o("pe", 0)
        y_stats(0)
        y_stats(1)
        y_scaled(0)
        y_second(0)
        w_late(LATE + 1)
        y_scaled(1)
        wo_lo(2)
        wo_lo(3)
        w_late(LATE + 2)
        wy_t("pe", 0)
        wy_hi(0)
        w_load(2)
        o("pe", 1)
        y_second(1)
        wy_lo(0)
        wy_t("pe", 1)
        w_load(3)
        wy_hi(1)
        wo_mm("pe", 0)
        y_stats(2)
        y_stats(3)
        y_scaled(2)
        wy_lo(1)
        y_second(2)
        wo_mm("pe", 1, lambda: wy_t("pe", 2))
        wy_hi(2)
        x1(0)
        y_scaled(3)
        wy_lo(2)
        y_second(3)
        stats2(0)
        wo_mm("pe", 2, lambda: wy_t("pe", 3))
        wy_hi(3)
        w_load(4)
        w_load(5)
        x1(1)
        wy_lo(3)
        norm2(0)
        stats2(1)
        v_hi(2)
        wo_mm("pe", 3, lambda: x2_t("pe", 0))
        transposed_hi(("x2", 0), x2_dst(0)[0])
        x1(2)
        norm2(1)
        stats2(2)
        transposed_lo(("x2", 0), x2_dst(0)[1], x2_dst(0)[0])
        x2_t("pe", 1)
        transposed_hi(("x2", 1), x2_dst(1)[0])
        w_late(LATE + 3)
        x1(3)
        norm2(2)
        stats2(3)
        transposed_lo(("x2", 1), x2_dst(1)[1], x2_dst(1)[0])
        x2_t("pe", 2)
        transposed_hi(("x2", 2), x2_dst(2)[0])
        norm2(3)
        v_lo(2)
        x2_t("pe", 3)
        transposed_hi(("x2", 3), x2_dst(3)[0])
        o("pe", 2)
        transposed_lo(("x2", 2), x2_dst(2)[1], x2_dst(2)[0])
        transposed_lo(("x2", 3), x2_dst(3)[1], x2_dst(3)[0])
        dma(("dld", 0), f(down), down_s.rearrange("(i p) n -> p i n", p=128),
            [(f"scr{c}", 0) for c in range(8, 12)] + [("w", B - 1), ("v", B - 1), ("ad", 0)])
        do("dve", lambda e: e.tensor_scalar(ds, ds, tg[:, 1:2], None, ALU.mult), [("rows", 0), ("tg", 0)], ("ds", 0))

        for g in range(NG):
            nxt = g + 1 < NG
            for s in range(15):
                if nxt and (g or s):
                    att_pe("pe2", g + 1, s)
                if s < 11:
                    up_mm(g, s)
                else:
                    down_mm(g, s - 11)
                if nxt:
                    att_act(g + 1, s)
                if nxt and s in (1, 6):
                    y_second(4 * (g + 1) + (0 if s == 1 else 2))
                if 1 <= s <= 11:
                    hidden(g, s - 1)
                    hidden_hi(g, s - 1)
                if s < 11:
                    silu(g, s)
                if nxt:
                    att_dve(g + 1, s, False)
                if 1 <= s <= 11:
                    hidden_lo(g, s - 1)
                if s == 0 and g:
                    finish(4 * g - 1)
                    out_store(2 * g - 1)
                if s >= 12:
                    finish(4 * g + s - 12)
                if nxt:
                    att_dve(g + 1, s, True)
                    att_sp(g + 1, s)
                if s == 13:
                    out_store(2 * g)
                if s == 14 and not nxt:
                    dma(("outb", 0), out_v[:, 4 * g + 2, :], xr[:, (4 * g + 2) % 8, :], [("of", 4 * g + 2)])
        finish(4 * NG - 1)
        last = 4 * NG - 1
        dma(("out3", 2 * NG - 1), out_v[:, last, :], xr[:, last % 8, :], [("of", last)])
        do("sp", lambda e: None, [(f"out{q % 4}", q) for q in range(2 * NG - 4, 2 * NG)] + [("outb", 0)])

        sems = {kind: stack.enter_context(nc.semaphore(f"s_{kind}")) for kind in plan.total}
        block = stack.enter_context(nc.Block())

        @block.sync
        def _(e):
            plan.emit("sp", e, sems, {})

        @block.scalar
        def _(e):
            plan.emit("act", e, sems, {})

        @block.vector
        def _(e):
            plan.emit("dve", e, sems, {})

        @block.gpsimd
        def _(e):
            plan.emit("pool", e, sems, {})

        @block.tensor
        def _(e):
            seen = {}
            plan.emit("pe", e, sems, seen)
            e.wait_ge(sems["flag"], plan.value[("flag", 0)])
            some_low = e.alloc_register("some_low")
            e.reg_load(some_low, flag[0:1, 0:1])
            with e.If_eq(some_low, 0):
                plan.emit("pe2", e, sems, dict(seen), True)
            with e.Else():
                plan.emit("pe2", e, sems, dict(seen), False)


def decay_t():
    gam = np.float32(1.0) - np.float32(2.0) ** (-5.0 - np.arange(H, dtype=np.float32))
    idx = np.arange(S, dtype=np.float32)
    expo = idx[None, :] - idx[:, None]
    m = np.where(expo[None] <= 0, gam[:, None, None].astype(np.float64) ** np.minimum(expo, 0)[None], 0.0)
    m = m / np.sqrt(m.sum(axis=-1))[:, None, :] / np.sqrt(float(HD))
    return np.ascontiguousarray(m.transpose(2, 0, 1).reshape(S, H * S).astype(np.float32))


def kernel(x, ctx_2048, g_xattn, g_ffn, L0_xattn_Wh, L0_xattn_wg_w, L0_xattn_wo_w, L0_xattn_gn_gamma, L0_xattn_gn_beta,
           L0_ffn_gate_w, L0_ffn_up_w, L0_ffn_down_w, L0_ffn_gate_s, L0_ffn_up_s, L0_ffn_down_s):
    import numpy as _np
    import concourse.bacc as _bacc
    from concourse import mybir as _mybir
    from concourse.bass_utils import run_bass_kernel_spmd as _run

    def laid(a):
        return _np.ascontiguousarray(a)

    c = {k: _np.asarray(v) for k, v in dict(
        x=x, ctx=ctx_2048, gx=g_xattn, gf=g_ffn, wh=L0_xattn_Wh, wg=L0_xattn_wg_w, wo=L0_xattn_wo_w,
        gamma=L0_xattn_gn_gamma, beta=L0_xattn_gn_beta, gw=L0_ffn_gate_w, uw=L0_ffn_up_w, dw=L0_ffn_down_w,
        gs=L0_ffn_gate_s, us=L0_ffn_up_s, ds=L0_ffn_down_s).items()}
    arrays = {
        "in_x": laid(c["x"]),
        "in_ctx_t": laid(c["ctx"].transpose(2, 0, 1).reshape(D, B * S)),
        "in_wh": laid(c["wh"]),
        "in_wh_t": laid(c["wh"].transpose(0, 2, 1)),
        "in_wg": laid(c["wg"]),
        "in_wo": laid(c["wo"]),
        "in_gate_t": laid(c["gw"].T),
        "in_up_t": laid(c["uw"].T),
        "in_down_t": laid(c["dw"].T),
        "in_cols": laid(_np.concatenate([c["gs"].reshape(NI, 128).T, c["us"].reshape(NI, 128).T,
                                         _np.broadcast_to(c["gx"][0:1], (128, 1)),
                                         _np.broadcast_to(c["gf"][0:1], (128, 1))], axis=1)),
        "in_rows": laid(_np.broadcast_to(_np.stack([c["gamma"], c["beta"], c["ds"]]), (128, 3, D))),
        "in_decay": decay_t(),
        "in_eye": _np.eye(128, dtype=_np.float32),
    }
    nc = _bacc.Bacc("TRN2", target_bir_lowering=False, num_devices=1)
    args = [nc.dram_tensor(n, a.shape, _mybir.dt.from_np(a.dtype), kind="ExternalInput").ap() for n, a in arrays.items()]
    args.append(nc.dram_tensor("out", (B, S, D), _mybir.dt.float32, kind="ExternalOutput").ap())
    gated_layer(nc, *args)
    r = _run(nc, [arrays], core_ids=[0])
    return r.results[0]["out"]
```
